# Optimizing a Trainium2 kernel written in Bass

```python
import numpy as np
import jax
import jax.numpy as jnp

def _softmax(x, axis=-1):
    return jax.nn.softmax(x, axis=axis)

def _gelu(x):
    return jax.nn.gelu(x, approximate=True)

def _silu(x):
    return jax.nn.silu(x)

def _sigmoid(x):
    return jax.nn.sigmoid(x)

def _layernorm(x, axis=-1, eps=1e-05):
    m = jnp.mean(x, axis=axis, keepdims=True)
    v = jnp.var(x, axis=axis, keepdims=True)
    return (x - m) / jnp.sqrt(v + eps)

def _scatter_add(tgt, idx, src, axis=0):
    return tgt.at[idx].add(src)

def _segment_sum(src, seg, n):
    return jax.ops.segment_sum(src, seg, n)
kernel_name = 'mk_flamingo_gated_d1_seqx_r4_0e168e'

def setup_inputs(seed: int=0):
    np.random.seed(seed)
    _w = jnp.asarray

    def _rec_inputs():
        import jax
        import jax.numpy as jnp
        _rk = jax.random.key(seed)
        x = 7.22e-05 + 1 * jax.random.normal(jax.random.fold_in(_rk, 1), (4, 1024, 256), jnp.float32)
        _lenS = 1024 - jax.random.randint(jax.random.fold_in(_rk, 7), (4,), 0, max(1, 1024 // 4) + 1, jnp.int32)
        _lenS2 = 77 - jax.random.randint(jax.random.fold_in(_rk, 8), (4,), 0, max(1, 77 // 4) + 1, jnp.int32)
        _ctx_1024P = jax.random.normal(jax.random.fold_in(_rk, 11), (4, 16, 256), jnp.float32)
        _ctx_1024c = jax.random.dirichlet(jax.random.fold_in(_rk, 511), 0.3 * jnp.ones((16,), jnp.float32), (4, 77))
        _ctx_1024t = jnp.einsum('bsk,bkd->bsd', _ctx_1024c, _ctx_1024P)
        _ctx_1024t = _ctx_1024t * jax.lax.rsqrt(jnp.mean(jnp.square(_ctx_1024t)) + 1e-12) * 0.953939
        ctx_1024 = 4.13588e-05 + 0.999923 * (_ctx_1024t + 0.3 * jax.random.normal(jax.random.fold_in(_rk, 611), (4, 77, 256), jnp.float32))
        _validS = jnp.arange(1024)[None, :] < _lenS[:, None]
        _validS2 = jnp.arange(77)[None, :] < _lenS2[:, None]
        _causal = jnp.tril(jnp.ones((1024, 1024), dtype=bool))
        mask_BxS2_if1 = jnp.where(jnp.ones((4, 77), dtype=bool), 1, 0).astype(jnp.int32)
        _g = jax.random.normal(jax.random.fold_in(_rk, 9001), (2, 1), jnp.float32)
        _g = jnp.sign(_g) * jnp.maximum(jnp.abs(_g), 1.0) + (_g == 0) * 1.0
        g_xattn = _g[0]
        g_ffn = _g[1]
        return (x, ctx_1024, mask_BxS2_if1, g_xattn, g_ffn)
    x, ctx_1024, mask_BxS2_if1, g_xattn, g_ffn = _rec_inputs()

    def _L0_xattn_setup():
        import jax, jax.numpy as jnp
        import numpy as np
        D_MODEL = 256
        NUM_HEADS = 16
        D_KEY = D_MODEL // NUM_HEADS
        MASK_FUTURE = True
        NEG_INF = -jnp.inf
        key = jax.random.key(seed)
        ks = jax.random.split(key, 7)
        B, N = (4, 512)
        return {'query': jax.random.normal(ks[0], (B, N, D_MODEL), dtype=jnp.float32), 'key': jax.random.normal(ks[1], (B, N, D_MODEL), dtype=jnp.float32), 'value': jax.random.normal(ks[2], (B, N, D_MODEL), dtype=jnp.float32), 'mask': jnp.ones((B, N), dtype=jnp.int32), 'Wq': jax.random.normal(ks[3], (D_MODEL, D_MODEL), dtype=jnp.float32) * 0.02, 'Wk': jax.random.normal(ks[4], (D_MODEL, D_MODEL), dtype=jnp.float32) * 0.02, 'Wv': jax.random.normal(ks[5], (D_MODEL, D_MODEL), dtype=jnp.float32) * 0.02, 'Wo': jax.random.normal(ks[6], (D_MODEL, D_MODEL), dtype=jnp.float32) * 0.02}
    _L0_xattn_all = _L0_xattn_setup()
    _L0_xattn_in = {k: v for k, v in _L0_xattn_all.items() if k in ('Wq', 'Wk', 'Wv', 'Wo')}
    del _L0_xattn_all

    def _L0_ffn_setup():
        import jax, jax.numpy as jnp
        import numpy as np
        CAP_FACTOR = 1.5
        key = jax.random.key(seed)
        ks = jax.random.split(key, 6)
        E, S, D, M = (48, 4, 256, 256)
        K = D // S
        x = jax.random.normal(ks[0], (4, 1024, D), dtype=jnp.float32)
        Wr = jax.random.normal(ks[1], (E, D), dtype=jnp.float32) * 0.02
        W1 = jax.random.normal(ks[2], (E, S, D, M), dtype=jnp.float32) * (1.0 / np.sqrt(D))
        b1 = jnp.zeros((E, S, M), dtype=jnp.float32)
        W2 = jax.random.normal(ks[3], (E, S, M, K), dtype=jnp.float32) * (1.0 / np.sqrt(M))
        b2 = jnp.zeros((E, S, K), dtype=jnp.float32)
        return {'x': x, 'Wr': Wr, 'W1': W1, 'b1': b1, 'W2': W2, 'b2': b2}
    _L0_ffn_all = _L0_ffn_setup()
    _L0_ffn_in = {k: v for k, v in _L0_ffn_all.items() if k in ('Wr', 'W1', 'b1', 'W2', 'b2')}
    del _L0_ffn_all
    return {'x': x, 'ctx_1024': ctx_1024, 'mask_BxS2_if1': mask_BxS2_if1, 'g_xattn': g_xattn, 'g_ffn': g_ffn, 'L0_xattn_Wq': _L0_xattn_in['Wq'], 'L0_xattn_Wk': _L0_xattn_in['Wk'], 'L0_xattn_Wv': _L0_xattn_in['Wv'], 'L0_xattn_Wo': _L0_xattn_in['Wo'], 'L0_ffn_Wr': _L0_ffn_in['Wr'], 'L0_ffn_W1': _L0_ffn_in['W1'], 'L0_ffn_b1': _L0_ffn_in['b1'], 'L0_ffn_W2': _L0_ffn_in['W2'], 'L0_ffn_b2': _L0_ffn_in['b2']}

def reference(x, ctx_1024, mask_BxS2_if1, g_xattn, g_ffn, L0_xattn_Wq, L0_xattn_Wk, L0_xattn_Wv, L0_xattn_Wo, L0_ffn_Wr, L0_ffn_W1, L0_ffn_b1, L0_ffn_W2, L0_ffn_b2):
    import jax
    import jax.numpy as jnp

    def _L0_xattn_ref(query, key, value, mask, Wq, Wk, Wv, Wo):
        import jax, jax.numpy as jnp
        import numpy as np
        D_MODEL = 256
        NUM_HEADS = 16
        D_KEY = D_MODEL // NUM_HEADS
        MASK_FUTURE = True
        NEG_INF = -jnp.inf
        B, Nq, _ = query.shape
        Nk = key.shape[1]

        def proj(x, W, N):
            return (x @ W).reshape(B, N, NUM_HEADS, D_KEY).transpose(0, 2, 1, 3)
        Q = proj(query, Wq, Nq)
        K = proj(key, Wk, Nk)
        V = proj(value, Wv, Nk)
        scores = jnp.einsum('bhqd,bhkd->bhqk', Q, K) / np.sqrt(D_KEY).astype(np.float32)
        scores = jnp.where(mask[:, None, None, :] == 0, NEG_INF, scores)
        if MASK_FUTURE:
            causal = jnp.triu(jnp.ones((Nq, Nk), dtype=jnp.bool_), k=1)
            scores = jnp.where(causal[None, None, :, :], NEG_INF, scores)
        attn = jax.nn.softmax(scores, axis=-1)
        out = jnp.einsum('bhqk,bhkd->bhqd', attn, V)
        out = out.transpose(0, 2, 1, 3).reshape(B, Nq, D_MODEL)
        return out @ Wo

    def _L0_ffn_ref(x, Wr, W1, b1, W2, b2):
        import jax, jax.numpy as jnp
        import numpy as np
        CAP_FACTOR = 1.5
        orig_shape = x.shape
        D = x.shape[-1]
        E = Wr.shape[0]
        xf = x.reshape(-1, D)
        T = xf.shape[0]
        cap = int(CAP_FACTOR * T / E)
        logits = xf @ Wr.T
        vals, idx = jax.lax.top_k(logits.T, cap)
        w = jax.nn.softmax(vals, axis=-1)
        xg = xf[idx]
        h = jax.nn.gelu(jnp.einsum('ecd,esdm->ecsm', xg, W1) + b1[:, None], approximate=False)
        y = jnp.einsum('ecsm,esmk->ecsk', h, W2) + b2[:, None]
        y = y.reshape(E, cap, D) * w[..., None]
        out = jnp.zeros_like(xf).at[idx.reshape(-1)].add(y.reshape(-1, D))
        return out.reshape(orig_shape)
    x = x + jnp.tanh(g_xattn[0]) * _L0_xattn_ref(_layernorm(x, axis=-1), ctx_1024, ctx_1024, mask_BxS2_if1, L0_xattn_Wq, L0_xattn_Wk, L0_xattn_Wv, L0_xattn_Wo)
    x = x + jnp.tanh(g_ffn[0]) * _L0_ffn_ref(_layernorm(x, axis=-1), L0_ffn_Wr, L0_ffn_W1, L0_ffn_b1, L0_ffn_W2, L0_ffn_b2)
    return x

_drawn_inputs = setup_inputs


def setup_inputs(seed=0):
    import zlib

    import numpy as np

    out = dict(_drawn_inputs(seed))
    spreads = {'L0_ffn_b1': (0.0, 0.8), 'L0_ffn_b2': (0.0, 0.8)}
    factors = {'L0_xattn_Wq': 8.0, 'L0_xattn_Wk': 8.0, 'L0_ffn_Wr': 2.902}
    for name, (base, spread) in spreads.items():
        noise = np.random.default_rng([zlib.crc32(name.encode()), seed]).standard_normal(out[name].shape)
        drawn = base * np.exp(spread * noise) if base else spread * noise
        out[name] = jnp.asarray(drawn.astype(out[name].dtype))
    for name, factor in factors.items():
        out[name] = (out[name] * factor).astype(out[name].dtype)
    return out
```

```python
from contextlib import ExitStack

import concourse.bass as bass
from concourse import mybir

F32 = mybir.dt.float32
BF16 = mybir.dt.bfloat16
I32 = mybir.dt.int32
U32 = mybir.dt.uint32
ALU = mybir.AluOpType
ACT = mybir.ActivationFunctionType
AX = mybir.AxisListType
one = bass.ds

P = 128
B, N, D = 4, 1024, 256
NK = 77
H, DK = 16, 16
DV = DK + 1
E, S, M, KO = 48, 4, 256, 64
KC = D // P
TOK = B * N
NT = TOK // P
CAP = int(1.5 * TOK / E)
EPS = 1e-5
HH = H // KC
FLAT = HH * NK
BANKS = ((0, 5), (5, 10), (10, 16))
CH = 124
NCH = -(-FLAT // CH)
HALF = N // 2
G2 = 64
LP = G2 + E
ROUNDS = CAP // 8
NL = 2 * B
W = 8
LOOPS = E // W
NM = S * 2
MASKED = -1e30
TAKEN = -3e38
GROUPS = ((0, 4), (4, 8), (8, 10))
PIECES = (((0, 5),), ((5, 8), (8, 10)), ((10, 16),))
WIDE = 5
TLAG, SLAG, DLAG, OLAG, GLAG = 1, 2, 3, 4, 5
FIRST_PAIR, LAST_PAIR = 4, NT // 2
PICK = 14
LAST_STEP = PICK + (B - 1) * 8
META = 6
AHEAD = 3

V_BIAS = 3
V_CTX = V_BIAS + B + KC
V_KEYS = V_CTX + HH
V_VALUES = V_KEYS + 2 * B
V_BLOCKS = V_VALUES + KC * NCH
V_PARAMS = V_BLOCKS + 2
C_IDENT, C_SHIFTED, C_HEADS, C_ALL = 2, 4, 7, 14
A_GATE = 1
A_KEYS = A_GATE + HH
MERGE_MAX, MERGE_PLACE, MERGE_TABLE = 38, 70, 74


def chunk(i):
    a = CH * i
    n = min(CH, FLAT - a)
    return a, n, a // NK, (a + n - 1) // NK - a // NK + 1


def there(k, lag):
    return not isinstance(k, int) or 0 <= k - lag < NT


def past(t, back):
    return not isinstance(t, int) or t >= back


def apart(eng, s, value):
    value = value if isinstance(value, int) else eng.to_reg(value)
    eng.wait_ge(s["ready"], 1)
    return value


def build(nc, x, ctx_in, mask, g_xattn, g_ffn, Wq, Wk, Wv, Wo, Wr, W1, b1, W2, b2, out):
    normed = nc.dram_tensor("normed", [TOK, D], F32, kind="Internal").ap()
    table = nc.dram_tensor("table", [E * NL * CAP, 2], F32, kind="Internal").ap()
    out_rows = out.rearrange("b n d -> (b n) d")
    with ExitStack() as ctx:
        def sb(name, shape, dt=F32):
            return ctx.enter_context(nc.sbuf_tensor(name, shape, dt))

        score_ps = ctx.enter_context(nc.psum_tensor("score_ps", [P, 4, 512], F32))
        bank = [ctx.enter_context(nc.psum_tensor(f"bank{i}", [P, 512], F32)) for i in range(4)]
        names = """ready ctx_in wts_in small_in consts v_prep a_prep p_prep
            stat1 aggr1 var1 rstd1 xn_ready xT_ps xT_sb q_ps q_sb s_ps top_done s_sub p_exp pt_ps pt_sb pv_ps den_done
            o_ready oT_ps oT_sb y_ps x1_ready stat2 aggr2 var2 rstd2 x2_ready x2T_ps x2T_sb lg_ps lg_sb
            work_ready eight places taken filed out_stored merge exp_done turn table_stored slots_ready
            picked xg_ps xg_sb h_ps h_act y2_ps yb_done yo_ready scattered""".split()
        s = {n: ctx.enter_context(nc.semaphore(n)) for n in names}
        x_in = [ctx.enter_context(nc.semaphore(f"x_in{i}")) for i in range(NL)]
        x2_stored = [ctx.enter_context(nc.semaphore(f"x2_stored{i}")) for i in range(2)]
        w_in = [ctx.enter_context(nc.semaphore(f"w_in{i}")) for i in range(W)]
        meta_in = [ctx.enter_context(nc.semaphore(f"meta_in{i}")) for i in range(W)]
        xg_in = [ctx.enter_context(nc.semaphore(f"xg_in{i}")) for i in range(4)]

        xall = sb("xall", [P, NT, D])
        wq, wk, wv, wo = (sb(n, [P, KC, D]) for n in ("wq", "wk", "wv", "wo"))
        kblk = sb("kblk", [P, B * KC, FLAT])
        vblk = sb("vblk", [CH, B, KC * NCH, 3 * DV])
        wrT = sb("wrT", [P, KC, E])
        b1T = sb("b1T", [P, E * S, 2])
        mask_col = sb("mask_col", [NK, B], I32)
        keep_col = sb("keep_col", [NK, B])
        bias_tab = sb("bias_tab", [P, 2 * B, NK], BF16)
        ident = sb("ident", [P, P])
        ident16 = sb("ident16", [P, P], BF16)
        head_of = sb("head_of", [P, HH])
        minus_half = sb("minus_half", [P, 1])
        gate_in = sb("gate_in", [P, 2])
        filler = sb("filler", [1, 4])
        gate = sb("gate", [P, 2])
        xn = sb("xn", [P, 2, D])
        xT = sb("xT", [P, 2, KC, P])
        qT = sb("qT", [P, 2, KC, P])
        prob = sb("prob", [P, 2, H * NK])
        probT = sb("probT", [P, 2, KC * NCH, P])
        early_t, early_p = probT[:].rearrange("p a q t -> p (a q t)"), prob[:].rearrange("p a f -> p (a f)")
        ctx_sb = early_t[0:NK, 0:B * D].rearrange("p (b d) -> p b d", b=B)
        ctxT = early_t[:, B * D:B * D + KC * B * NK].rearrange("p (c n) -> p c n", c=KC)
        vaug = early_p[0:NK, 0:B * H * DV].rearrange("p (b h d) -> p b h d", b=B, h=H)
        b1_sb = early_p[0:2 * E, B * H * DV:B * H * DV + 2 * M].rearrange("p (a m) -> p a m", a=2)
        wr_sb = early_p[0:E, B * H * DV + 2 * M:B * H * DV + 2 * M + D]
        shifted = early_p[0:NK, B * H * DV + 2 * M + D:B * H * DV + 2 * M + D + 2 * CH + NK]
        after = B * D + KC * B * NK
        row_bias, mask_f = (early_t[:, after + i * B * NK:after + (i + 1) * B * NK].rearrange("p (b k) -> p b k", b=B)
                            for i in range(2))
        mask_row = mask_f.bitcast(I32)
        top = sb("top", [P, 2, H])
        den = sb("den", [P, 2, H])
        o_sb = sb("o_sb", [P, 2, D])
        oT = sb("oT", [P, 2, KC, P])
        x2 = sb("x2", [P, 2, D])
        x2T = sb("x2T", [P, 2, KC, P])
        ln1 = [sb(f"ln1_{n}", [P, 2, w]) for n, w in (("st", 6), ("mv", 2), ("var", 1), ("rstd", 1))]
        ln2 = [sb(f"ln2_{n}", [P, 2, w]) for n, w in (("st", 6), ("mv", 2), ("var", 1), ("rstd", 1))]
        logit = sb("logit", [LP, HALF])
        work = sb("work", [LP, HALF])
        m8 = sb("m8", [LP, 2, 8])
        i8 = sb("i8", [LP, 2, 8], U32)
        lval = sb("lval", [LP, B * ROUNDS, 8])
        lidx = sb("lidx", [LP, B * ROUNDS, 8], U32)
        w1 = [sb(f"w1_{i}", [P, S, KC, M]) for i in range(W)]
        w2 = [sb(f"w2_{i}", [P, S, 2, KO]) for i in range(W)]
        b2r = [sb(f"b2r_{i}", [P, D]) for i in range(W)]
        slot_of = sb("slot_of", [P, E], U32)
        pick = sb("pick", [P, W], U32)
        meta = sb("meta", [P, W, 2])
        hT = probT[:, :, 0:NM, :]
        xg = [xn[:, 0, :], xn[:, 1, :]] + [qT[:, a].rearrange("p c t -> p (c t)") for a in range(2)]
        xgT, yb, yo = xT, o_sb, x2
        listbase_i = sb("listbase_i", [E, NL], I32)
        listbase = sb("listbase", [E, NL])
        slot_i = lval[0:E].rearrange("p r w -> p (r w)")[:, 0:CAP].bitcast(I32)
        slot_f = sb("slot_f", [E, CAP])
        row_i = sb("row_i", [E, 1], I32)
        row_f = sb("row_f", [E, 1])
        small = sb("small", [E, 16, NL])
        free = kblk[0:E].rearrange("p a f -> p (a f)")
        vals8, ids, flags = (free[:, i * NL * CAP:(i + 1) * NL * CAP].rearrange("p (l c) -> p l c", l=NL)
                             for i in range(3))
        sort_a, sort_b = (free[:, 3 * NL * CAP + i * 4 * CAP:3 * NL * CAP + (i + 1) * 4 * CAP] for i in range(2))
        expo = free[:, 4 * NL * CAP:4 * NL * CAP + CAP]
        tab = prob[0:E].rearrange("p a f -> p (a f)")[:, 0:NL * CAP * 2].rearrange("p (l c w) -> p l c w", l=NL, w=2)
        best_of, place_of = sort_a[:, 0:CAP], sort_b[:, 0:CAP]
        xpairs = xall[:].rearrange("p (n u) d -> p n u d", u=2)
        xt_ps, q_psum = bank[2][:, 0:D], bank[2][:, D:2 * D]
        ot_ps, y_psum = bank[3][:, 0:D], bank[3][:, D:2 * D]
        pv_psum, lg_psum = score_ps[:, 3, 0:H * DV], score_ps[:, 3, H * DV:H * DV + P]
        h_psum = [score_ps[:, 2 * v:2 * v + 2, :].rearrange("p a (m t) -> p (a m) t", t=P) for v in range(2)]

        def block_ps(q):
            c, i = divmod(q, NCH)
            _, n, _, nh = chunk(i)
            starts = [0, 0]
            for m in range(i):
                starts[m // 3] += B * DV * chunk(m)[3]
            a = starts[i // 3]
            return score_ps[0:n, 2 * c + i // 3, a:a + B * DV * nh].rearrange("p (b w) -> p b w", b=B)

        block = ctx.enter_context(nc.Block())

        @block.sync
        def _(sp):
            def load_x(b, u):
                sp.dma_start(xpairs[:, 4 * b:4 * b + 4, u, :],
                             x[b, u * HALF:(u + 1) * HALF, :].rearrange("(j p) d -> p j d", p=P)
                             ).then_inc(x_in[2 * b + u], 16)

            def load_weights(e, i):
                sp.dma_start(w1[i][:], W1[one(e, 1)][0].rearrange("s (p c) m -> p s c m", c=KC)).then_inc(w_in[i], 16)
                sp.dma_start(w2[i][:], W2[one(e, 1)][0].rearrange("s (p c) k -> p s c k", c=2)).then_inc(w_in[i], 16)
                sp.dma_start(b2r[i][:], b2[one(e, 1)].rearrange("a s k -> a (s k)").broadcast_to([P, D])
                             ).then_inc(w_in[i], 16)

            def store_normed(b, j, u):
                sp.wait_ge(s["x2_ready"], 8 * b + 2 * j + u + 1)
                sp.dma_start(normed[one((8 * b + j + 4 * u) * P, P)], x2[:, u, :]).then_inc(x2_stored[u], 16)

            sp.dma_start(ctx_sb, ctx_in.rearrange("b k d -> k b d")).then_inc(s["ctx_in"], 16)
            load_x(0, 0)
            for dst, src in ((wk, Wk), (wv, Wv), (wq, Wq), (wo, Wo)):
                sp.dma_start(dst[:], src.rearrange("(k p) n -> p k n", p=P)).then_inc(s["wts_in"], 16)
            for i in range(1, NL):
                load_x(i // 2, i % 2)
            for i in range(W):
                load_weights(i, i)
            with sp.Fori(0, B) as b:
                with sp.Fori(0, 4) as j:
                    store_normed(b, j, 0)
                    store_normed(b, j, 1)
                for u in range(2):
                    sp.dma_start(out[one(b, 1)][0][u * HALF:(u + 1) * HALF].rearrange("(j p) d -> p j d", p=P),
                                 xpairs[:, one(4 * b, 4), u, :]).then_inc(s["out_stored"], 16)
            with sp.Fori(1, LOOPS) as it:
                for i in range(W):
                    sp.wait_ge(s["y2_ps"], W * it + i - W + 1)
                    sp.wait_ge(s["yb_done"], W * it + i - W + 1)
                    load_weights(W * it + i, i)
            sp.wait_ge(s["out_stored"], 16 * 2 * B)

        @block.gpsimd
        def _(pool):
            made = [0]

            def make(ins):
                made[0] += 1
                ins.then_inc(s["consts"], 1)
                pool.wait_ge(s["consts"], made[0])

            def affine(t, compare, fill, base, pattern, channel):
                make(pool.affine_select(out=t, in_=t, compare_op=compare, fill=fill, base=base, pattern=pattern,
                                        channel_multiplier=channel))
            make(pool.memset(ident[:], 0.0))
            affine(ident[:], ALU.not_equal, 1.0, 0, [[-1, P]], 1)
            make(pool.memset(shifted, 0.0))
            affine(shifted, ALU.not_equal, 1.0, CH, [[-1, 2 * CH + NK]], 1)
            make(pool.memset(head_of[:], 1.0))
            affine(head_of[:], ALU.is_ge, 0.0, 0, [[-DK, HH]], 1)
            affine(head_of[:], ALU.is_ge, 0.0, DK - 1, [[DK, HH]], -1)
            make(pool.memset(minus_half[:], -0.5))
            make(pool.memset(logit[:], 0.0))
            for i, (n, by) in enumerate((("filed", 4), ("taken", 1), ("work_ready", 1), ("ready", 1))):
                pool.memset(filler[:, i:i + 1], 0.0).then_inc(s[n], by)
            make(pool.tensor_copy(ident16[:], ident[:]))
            pool.wait_ge(s["v_prep"], V_BIAS)
            for b in range(B):
                make(pool.affine_select(out=bias_tab[:, 2 * b, :], in_=row_bias[:, b, :], compare_op=ALU.is_ge,
                                        fill=MASKED, base=0, pattern=[[-1, NK]], channel_multiplier=1))
            assert made[0] == C_ALL
            make(pool.iota(listbase_i[:], pattern=[[HALF, NL]], base=0, channel_multiplier=0))
            make(pool.iota(slot_i, pattern=[[1, CAP]], base=0, channel_multiplier=0))
            make(pool.iota(row_i[:], pattern=[[0, 1]], base=0, channel_multiplier=NL * CAP))
            make(pool.tensor_copy(listbase[:], listbase_i[:]))
            make(pool.tensor_copy(slot_f[:], slot_i))
            make(pool.tensor_copy(row_f[:], row_i[:]))

            def rstd(t, u, ln, ready, mid, done):
                _, mv, var, to = ln
                pool.wait_ge(s[ready], apart(pool, s, t + 1))
                pool.tensor_scalar(var[:, u, :], mv[:, u, 1:2], EPS, None, ALU.add).then_inc(s[mid], 1)
                pool.wait_ge(s[mid], t + 1)
                pool.tensor_tensor(to[:, u, :], var[:, u, :], minus_half[:], ALU.pow).then_inc(s[done], 1)

            def file(r, rr):
                pool.wait_ge(s["places"], r + 1)
                pool.tensor_copy(lval[:, one(r, 1), :], m8[:, rr:rr + 1, :]).then_inc(s["filed"], 1)
                pool.tensor_copy(lidx[:, one(r, 1), :], i8[:, rr:rr + 1, :]).then_inc(s["filed"], 1)

            def step(k, u, picking):
                if there(k, 0):
                    rstd(k, u, ln1, "aggr1", "var1", "rstd1")
                if there(k, OLAG):
                    rstd(k - OLAG, (u + OLAG) % 2, ln2, "aggr2", "var2", "rstd2")
                if picking:
                    for rr in range(2):
                        file(2 * (k - PICK) + rr, rr)

            for k in range(2 * FIRST_PAIR):
                step(k, k % 2, False)
            with pool.Fori(FIRST_PAIR, PICK // 2) as n:
                for u in range(2):
                    step(2 * n + u, u, False)
            with pool.Fori(PICK // 2, LAST_PAIR) as n:
                for u in range(2):
                    step(2 * n + u, u, True)
            for k in range(NT, LAST_STEP):
                step(k, k % 2, True)
            with pool.Fori((B - 1) * ROUNDS // 2, B * ROUNDS // 2) as n:
                for rr in range(2):
                    file(2 * n + rr, rr)

            def gather_meta(e, i):
                pool.tensor_copy(pick[:, i:i + 1], slot_of[:, one(e, 1)]).then_inc(s["picked"], 1)
                pool.wait_ge(s["picked"], apart(pool, s, e + 1))
                pool.indirect_dma_start(meta[:, i, :], None, table,
                                        bass.IndirectOffsetOnAxis(ap=pick[:, i:i + 1], axis=0)
                                        ).then_inc(meta_in[i], 16)

            def gather_tokens(e, uses, i):
                pool.wait_ge(meta_in[i], apart(pool, s, 16 * uses + 16))
                if past(e, 4):
                    pool.wait_ge(s["xg_ps"], apart(pool, s, e - 3))
                pool.indirect_dma_start(xg[i % 4], None, normed,
                                        bass.IndirectOffsetOnAxis(ap=meta[:, i, 0:1].bitcast(U32), axis=0)
                                        ).then_inc(xg_in[i % 4], 16)

            def scatter(e, i):
                pool.wait_ge(s["yo_ready"], apart(pool, s, e + 1))
                if past(e, 1):
                    pool.wait_ge(s["scattered"], apart(pool, s, 16 * e))
                pool.indirect_dma_start(out_rows, bass.IndirectOffsetOnAxis(ap=meta[:, i, 0:1].bitcast(U32), axis=0),
                                        yo[:, i % 2, :], None, compute_op=ALU.add).then_inc(s["scattered"], 16)

            def expert(it, i, last):
                e = W * it + i
                if not last or i + AHEAD < W:
                    gather_tokens(e + AHEAD, it + (i + AHEAD) // W, (i + AHEAD) % W)
                scatter(e, i)
                if not last or i + META < W:
                    gather_meta(e + META, (i + META) % W)

            pool.wait_ge(s["slots_ready"], 1)
            pool.wait_ge(s["table_stored"], 16)
            for u in range(2):
                pool.wait_ge(x2_stored[u], 16 * NT // 2)
            pool.wait_ge(s["out_stored"], 16 * 2 * B)
            for e in range(META):
                gather_meta(e, e)
            for e in range(AHEAD):
                gather_tokens(e, 0, e)
            for i in range(W):
                expert(0, i, False)
            with pool.Fori(1, LOOPS - 1) as it:
                for i in range(W):
                    expert(it, i, False)
            for i in range(W):
                expert(LOOPS - 1, i, True)
            pool.wait_ge(s["scattered"], 16 * E)

        @block.vector
        def _(dve):
            prep = [0]

            def link(ins):
                prep[0] += 1
                ins.then_inc(s["v_prep"], 1)
                dve.wait_ge(s["v_prep"], prep[0])
            link(dve.memset(bank[1][:], 0.0))
            dve.wait_ge(s["small_in"], 16 * 6)
            link(dve.tensor_scalar(keep_col[:], mask_col[:], 0.0, None, ALU.not_equal))
            link(dve.tensor_scalar(row_bias, mask_row, 0.0, MASKED, ALU.is_equal, ALU.mult))
            for b in range(B):
                link(dve.tensor_copy(bias_tab[:, 2 * b + 1, :], row_bias[:, b, :]))
            dve.wait_ge(s["p_prep"], 1)
            for c in range(KC):
                link(dve.tensor_copy(ctxT[:, c, :], score_ps[:, c, 0:B * NK]))
            assert prep[0] == V_CTX
            dve.wait_ge(s["p_prep"], 2)
            dve.wait_ge(s["consts"], C_HEADS)
            keys = kblk[:].rearrange("p (b c) (h k) -> p b c h k", c=KC, h=HH)
            for h in range(HH):
                link(dve.tensor_scalar(keys[:, :, 0, h, :], score_ps[:, 2, 0:B * NK].rearrange("p (b k) -> p b k", b=B),
                                       head_of[:, h:h + 1], None, ALU.mult))
            dve.wait_ge(s["p_prep"], 3)
            for b in range(B):
                link(dve.tensor_scalar(vaug[:, b, :, 0:DK], bank[b][0:NK, 0:D].rearrange("p (h d) -> p h d", h=H),
                                       keep_col[:, b:b + 1], None, ALU.mult))
                link(dve.tensor_copy(vaug[:, b, :, DK:DV],
                                     keep_col[:, b:b + 1].broadcast_to([NK, H])))
            assert prep[0] == V_VALUES
            dve.wait_ge(s["p_prep"], 4)
            for q in range(KC * NCH):
                _, n, _, nh = chunk(q % NCH)
                link(dve.tensor_copy(vblk[0:n, :, q, 0:nh * DV], block_ps(q)))
            dve.wait_ge(s["p_prep"], 5)
            link(dve.tensor_copy(wrT[:], bank[2][:, 0:KC * E].rearrange("p (c e) -> p c e", c=KC)))
            link(dve.tensor_copy(b1T[:].rearrange("p n c -> p c n"),
                                 bank[3][:, 0:2 * E * S].rearrange("p (c n) -> p c n", c=2)))
            assert prep[0] == V_PARAMS
            dve.wait_ge(s["a_prep"], A_GATE)

            def stats(t, u, ln, stat, aggr):
                st, mv, _, _ = ln
                dve.bn_stats(st[:, u, :], xall[:, one(t, 1), :]).then_inc(s[stat], 1)
                dve.wait_ge(s[stat], apart(dve, s, t + 1))
                dve.bn_aggr(mv[:, u, :], st[:, u, :]).then_inc(s[aggr], 1)

            def normalise(t, u, ln, to, rstd, done):
                dve.wait_ge(s[rstd], t + 1)
                dve.tensor_scalar(to[:, u:u + 1, :], xall[:, one(t, 1), :], ln[1][:, u, 0:1], ln[3][:, u, :],
                                  ALU.subtract, ALU.mult).then_inc(s[done], 1)

            def step(k, u, picking):
                if there(k, SLAG):
                    t, v = k - SLAG, (u + SLAG) % 2
                    sc = score_ps[:, 0:3, 0:WIDE * NK].rearrange("p q (h k) -> p q h k", h=WIDE)
                    last = score_ps[:, 2:3, WIDE * NK:(WIDE + 1) * NK]
                    p = prob[:, v, :].rearrange("p (h k) -> p h k", k=NK)
                    dve.wait_ge(s["s_ps"], t + 1)
                    dve.tensor_reduce(top[:, v, 0:H - 1].rearrange("p (q h) -> p q h", q=3), sc, AX.X, ALU.max
                                      ).then_inc(s["top_done"], 1)
                    dve.tensor_reduce(top[:, v, H - 1:H], last, AX.X, ALU.max).then_inc(s["top_done"], 1)
                    dve.wait_ge(s["top_done"], 2 * t + 2)
                    if past(t, 2):
                        dve.wait_ge(s["pt_ps"], 3 * (t - 1))
                    dve.tensor_tensor(p[:, 0:H - 1, :].rearrange("p (q h) k -> p q h k", q=3), sc,
                                      top[:, v, 0:H - 1].rearrange("p (q h a) -> p q h a", q=3, a=1)
                                      .broadcast_to([P, 3, WIDE, NK]), ALU.subtract).then_inc(s["s_sub"], 1)
                    dve.tensor_tensor(p[:, H - 1:H, :], last, top[:, v:v + 1, H - 1:H].broadcast_to([P, 1, NK]),
                                      ALU.subtract).then_inc(s["s_sub"], 1)
                if there(k, 0):
                    if isinstance(k, int) and k < 2:
                        dve.wait_ge(x_in[k], 16)
                    stats(k, u, ln1, "stat1", "aggr1")
                if there(k, DLAG):
                    t, v = k - DLAG, (u + DLAG) % 2
                    pv = pv_psum.rearrange("p (h d) -> p h d", d=DV)
                    inverse = den[:, v, :].rearrange("p (h a) -> p h a", a=1)
                    dve.wait_ge(s["pv_ps"], t + 1)
                    dve.reciprocal(inverse, pv[:, :, DK:DV]).then_inc(s["den_done"], 1)
                    dve.wait_ge(s["den_done"], t + 1)
                    if past(t, 2):
                        dve.wait_ge(s["oT_ps"], t - 1)
                    dve.tensor_tensor(o_sb[:, v, :].rearrange("p (h d) -> p h d", d=DK), pv[:, :, 0:DK],
                                      inverse.broadcast_to([P, H, DK]), ALU.mult).then_inc(s["o_ready"], 1)
                if there(k, OLAG):
                    t, v = k - OLAG, (u + OLAG) % 2
                    dve.wait_ge(s["y_ps"], t + 1)
                    dve.scalar_tensor_tensor(out=xall[:, one(t, 1), :], in0=y_psum.rearrange("p (a d) -> p a d", a=1),
                                             scalar=gate[:, 0:1], in1=xall[:, one(t, 1), :], op0=ALU.mult,
                                             op1=ALU.add).then_inc(s["x1_ready"], 1)
                    dve.wait_ge(s["x1_ready"], apart(dve, s, t + 1))
                    stats(t, v, ln2, "stat2", "aggr2")
                if there(k, 0):
                    if past(k, 2):
                        dve.wait_ge(s["xT_ps"], k - 1)
                    normalise(k, u, ln1, xn, "rstd1", "xn_ready")
                if there(k, OLAG):
                    t, v = k - OLAG, (u + OLAG) % 2
                    if past(t, 2):
                        dve.wait_ge(s["x2T_ps"], t - 1)
                        dve.wait_ge(x2_stored[v], 8 * (t - v))
                    normalise(t, v, ln2, x2, "rstd2", "x2_ready")
                if picking:
                    for rr in range(2):
                        pick_eight(2 * (k - PICK) + rr, rr)

            def take_logits(b):
                dve.wait_ge(s["lg_sb"], 8 * b + 8)
                if past(b, 1):
                    dve.wait_ge(s["taken"], ROUNDS * b + 1)
                dve.tensor_copy(work[:], logit[:]).then_inc(s["work_ready"], 1)
                dve.wait_ge(s["work_ready"], apart(dve, s, b + 2))

            def pick_eight(r, rr):
                if past(r, 1):
                    dve.wait_ge(s["taken"], apart(dve, s, r + 1))
                dve.wait_ge(s["filed"], apart(dve, s, 2 * r + 2))
                dve.max(m8[:, rr, :], work[:]).then_inc(s["eight"], 1)
                dve.wait_ge(s["eight"], apart(dve, s, r + 1))
                dve.max_index(i8[:, rr, :], m8[:, rr, :], work[:]).then_inc(s["places"], 1)
                dve.wait_ge(s["places"], apart(dve, s, r + 1))
                dve.match_replace(work[:], m8[:, rr, :], work[:], TAKEN).then_inc(s["taken"], 1)

            for k in range(2 * FIRST_PAIR):
                step(k, k % 2, False)
            for i in range(2, NL):
                dve.wait_ge(x_in[i], 16)
            with dve.Fori(FIRST_PAIR, PICK // 2) as n:
                for u in range(2):
                    step(2 * n + u, u, False)
            with dve.Fori(0, 2) as b:
                take_logits(b)
                with dve.Fori(0, 4) as j:
                    for u in range(2):
                        step(8 * b + 2 * j + PICK + u, u, True)
            take_logits(2)
            for k in range(PICK + 16, LAST_STEP):
                step(k, k % 2, True)
            take_logits(3)
            with dve.Fori((B - 1) * ROUNDS // 2, B * ROUNDS // 2) as n:
                for rr in range(2):
                    pick_eight(2 * n + rr, rr)

            merged = [0]

            def then(ins):
                merged[0] += 1
                ins.then_inc(s["merge"], 1)
                dve.wait_ge(s["merge"], merged[0])
            dve.wait_ge(s["filed"], 2 * B * ROUNDS + 4)
            dve.wait_ge(s["consts"], C_ALL + 6)
            listed = vals8[:]
            for g in range(2):
                lv = lval[G2 * g:G2 * g + E].rearrange("p (b r) w -> p b (r w)", b=B)
                li = lidx[G2 * g:G2 * g + E].rearrange("p (b r) w -> p b (r w)", b=B)
                then(dve.tensor_copy(listed[:, g::2, :], lv))
                then(dve.tensor_copy(ids[:, g::2, :], li))
            A_, B_ = sort_a[:], sort_b[:]

            def sort(n):
                a, b = A_, B_
                w = CAP // 2
                while w:
                    av = a[:, 0:n * CAP].rearrange("p (m t w) -> p m t w", t=2, w=w)
                    bv = b[:, 0:n * CAP].rearrange("p (m t w) -> p m t w", t=2, w=w)
                    dve.tensor_tensor(bv[:, :, 0, :], av[:, :, 0, :], av[:, :, 1, :], ALU.max).then_inc(s["merge"], 1)
                    merged[0] += 1
                    then(dve.tensor_tensor(bv[:, :, 1, :], av[:, :, 0, :], av[:, :, 1, :], ALU.min))
                    a, b = b, a
                    w //= 2
                return a, b

            def halve(to, lists):
                n = lists.shape[1] // 2
                then(dve.tensor_tensor(to[:, 0:n * CAP].rearrange("p (n c) -> p n c", n=n), lists[:, 0::2, :],
                                       lists[:, 1::2, ::-1], ALU.max))
            halve(A_, listed)
            a, b = sort(4)
            halve(b, a[:, 0:4 * CAP].rearrange("p (n c) -> p n c", n=4))
            A_, B_ = b, a
            a, b = sort(2)
            halve(b, a[:, 0:2 * CAP].rearrange("p (n c) -> p n c", n=2))
            best, place = best_of, place_of
            least, most, nmost, need, zsum, wz = (small[:, 12 + i // NL, i % NL:i % NL + 1] for i in range(6))
            gt, ge, eq, before, avail, take, upto, rest = (small[:, i, :] for i in range(8))
            then(dve.tensor_reduce(least, best, AX.X, ALU.min))
            then(dve.tensor_reduce(most, listed[:, :, 0], AX.X, ALU.max))
            then(dve.tensor_scalar(nmost, most, -1.0, None, ALU.mult))
            assert merged[0] == MERGE_MAX or print("MERGE_MAX", merged[0]) is None
            for to, op in ((gt, ALU.is_gt), (ge, ALU.is_ge)):
                then(dve.tensor_scalar(flags[:], listed, least, None, op))
                then(dve.tensor_reduce(to, flags[:], AX.X, ALU.add))
            then(dve.tensor_tensor(eq, ge, gt, ALU.subtract))
            then(dve.tensor_reduce(need, gt, AX.X, ALU.add))
            then(dve.tensor_scalar(need, need, -1.0, float(CAP), ALU.mult, ALU.add))

            def prefix(to, of, inclusive):
                if inclusive:
                    then(dve.tensor_copy(to[:, 0:1], of[:, 0:1]))
                else:
                    then(dve.memset(to[:, 0:1], 0.0))
                for i in range(1, NL):
                    then(dve.tensor_tensor(to[:, i:i + 1], to[:, i - 1:i], of[:, i - 1 + inclusive:i + inclusive],
                                           ALU.add))
            prefix(before, eq, 0)
            then(dve.tensor_scalar(avail, before, -1.0, need, ALU.mult, ALU.add))
            then(dve.tensor_scalar(avail, avail, 0.0, None, ALU.max))
            then(dve.tensor_tensor(take, avail, eq, ALU.min))
            then(dve.tensor_tensor(take, take, gt, ALU.add))
            prefix(upto, take, 1)
            then(dve.tensor_scalar(rest, take, -1.0, float(CAP), ALU.mult, ALU.add))
            fl = flags[:, 0:NL - 1, :]
            then(dve.tensor_tensor(fl, slot_f[:].rearrange("p (a c) -> p a c", a=1).broadcast_to([E, NL - 1, CAP]),
                                   upto[:, 0:NL - 1].rearrange("p (l a) -> p l a", a=1).broadcast_to([E, NL - 1, CAP]),
                                   ALU.is_ge))
            then(dve.tensor_tensor(fl, fl, rest[:, 0:NL - 1].rearrange("p (l a) -> p l a", a=1)
                                   .broadcast_to([E, NL - 1, CAP]), ALU.mult))
            then(dve.tensor_reduce(place, fl.rearrange("p l c -> p c l"), AX.X, ALU.add))
            then(dve.scalar_tensor_tensor(out=place, in0=place, scalar=row_f[:, 0:1], in1=slot_f[:], op0=ALU.add,
                                          op1=ALU.add))
            assert merged[0] == MERGE_PLACE or print("MERGE_PLACE", merged[0]) is None
            then(dve.tensor_tensor(tab[:, :, :, 0].bitcast(U32), ids[:],
                                   listbase[:].rearrange("p (l a) -> p l a", a=1).broadcast_to([E, NL, CAP]), ALU.add))
            dve.wait_ge(s["exp_done"], 2)
            then(dve.reciprocal(wz, zsum))
            then(dve.tensor_tensor(wz, wz, gate[0:E, 1:2], ALU.mult))
            then(dve.tensor_scalar(tab[:, :, :, 1], listed, wz, None, ALU.mult))
            assert merged[0] == MERGE_TABLE or print("MERGE_TABLE", merged[0]) is None
            dve.wait_ge(s["turn"], 1)
            dve.tensor_copy(slot_of[:], bank[0][:, 0:E]).then_inc(s["slots_ready"], 1)

            def turned(e, v):
                dve.wait_ge(s["xg_ps"], e + 1)
                dve.tensor_copy(xgT[:, v, :, :], bank[2][:, D * v:D * v + D].rearrange("p (c t) -> p c t", c=KC)
                                ).then_inc(s["xg_sb"], 1)

            def weigh(e, i):
                dve.wait_ge(s["y2_ps"], e + 1)
                dve.tensor_tensor(yb[:, i % 2, :], bank[3 - 2 * (i % 2)][:, 0:D], b2r[i][:], ALU.add
                                  ).then_inc(s["yb_done"], 1)
                dve.wait_ge(s["yb_done"], e + 1)
                if past(e, 2):
                    dve.wait_ge(s["scattered"], 16 * (e - 1))
                dve.tensor_scalar(yo[:, i % 2, :], yb[:, i % 2, :], meta[:, i, 1:2], None, ALU.mult
                                  ).then_inc(s["yo_ready"], 1)

            def expert(it, i, last):
                if not last or i + 1 < W:
                    turned(W * it + i + 1, (i + 1) % 2)
                weigh(W * it + i, i)
            turned(0, 0)
            for i in range(W):
                expert(0, i, False)
            with dve.Fori(1, LOOPS - 1) as it:
                for i in range(W):
                    expert(it, i, False)
            for i in range(W):
                expert(LOOPS - 1, i, True)

        @block.scalar
        def _(act):
            for dst, src in ((mask_row, mask.rearrange("(a b) k -> a b k", a=1).broadcast_to([P, B, NK])),
                             (mask_col[:].rearrange("p (b a) -> p b a", a=1), mask.rearrange("b (k a) -> k b a", a=1)),
                             (gate_in[:, 0:1], g_xattn.rearrange("(a b) -> a b", a=1).broadcast_to([P, 1])),
                             (gate_in[:, 1:2], g_ffn.rearrange("(a b) -> a b", a=1).broadcast_to([P, 1])),
                             (wr_sb, Wr),
                             (b1_sb, b1.rearrange("e s m -> (e s) m").rearrange("(a p) m -> p a m", a=2))):
                act.dma_start(dst, src, allow_slow_non_contiguous=True).then_inc(s["small_in"], 16)
            act.preload_act_table(ACT.Exp)
            act.wait_ge(s["small_in"], 16 * 6)
            act.activation(gate[:], gate_in[:], ACT.Tanh).then_inc(s["a_prep"], 1)
            act.wait_ge(s["p_prep"], 2)
            act.wait_ge(s["consts"], C_HEADS)
            keys = kblk[:].rearrange("p (b c) (h k) -> p b c h k", c=KC, h=HH)
            for h in range(HH):
                act.activation(keys[:, :, 1, h, :], score_ps[:, 3, 0:B * NK].rearrange("p (b k) -> p b k", b=B),
                               ACT.Copy, scale=head_of[:, h:h + 1]).then_inc(s["a_prep"], 1)

            def step(k, u):
                def turn_out(t, v, ready, src, dst, done, scale=1.0):
                    act.wait_ge(s[ready], t + 1)
                    act.activation(dst[:, v, :, :], src.rearrange("p (c t) -> p c t", c=KC), ACT.Copy, scale=scale
                                   ).then_inc(s[done], 1)

                def probs_out(g):
                    t, v = k - DLAG, (u + DLAG) % 2
                    q0, q1 = GROUPS[g]
                    act.wait_ge(s["pt_ps"], 3 * t + g + 1)
                    act.activation(probT[0:CH, v, q0:q1, :], bank[g % 2][0:CH, 0:P * (q1 - q0)]
                                   .rearrange("p (q t) -> p q t", t=P), ACT.Copy).then_inc(s["pt_sb"], 1)
                if there(k, TLAG):
                    turn_out(k - TLAG, (u + TLAG) % 2, "xT_ps", xt_ps, xT, "xT_sb")
                if there(k, DLAG):
                    probs_out(0)
                    probs_out(1)
                if there(k, TLAG):
                    turn_out(k - TLAG, (u + TLAG) % 2, "q_ps", q_psum, qT, "q_sb", DK ** -0.5)
                if there(k, DLAG):
                    probs_out(2)
                if there(k, OLAG):
                    turn_out(k - OLAG, (u + OLAG) % 2, "oT_ps", ot_ps, oT, "oT_sb")
                if there(k, GLAG):
                    turn_out(k - GLAG, (u + GLAG) % 2, "x2T_ps", xt_ps, x2T, "x2T_sb")
                if there(k, SLAG):
                    t, v = k - SLAG, (u + SLAG) % 2
                    act.wait_ge(s["s_sub"], 2 * t + 2)
                    act.activation(prob[:, v, :], prob[:, v, :], ACT.Exp).then_inc(s["p_exp"], 1)
                if there(k, GLAG):
                    t, v = k - GLAG, (u + GLAG) % 2
                    act.wait_ge(s["lg_ps"], t + 1)
                    if past(t, 8):
                        act.wait_ge(s["work_ready"], t // 8 + 1)
                    j = t // 2 % 4
                    act.activation(logit[G2 * v:G2 * v + E, one(j * P, P)], lg_psum[G2 * v:G2 * v + E, :], ACT.Copy
                                   ).then_inc(s["lg_sb"], 1)
            for k in range(2 * FIRST_PAIR):
                step(k, k % 2)
            with act.Fori(FIRST_PAIR, LAST_PAIR) as n:
                for u in range(2):
                    step(2 * n + u, u)
            for k in range(NT, NT + GLAG):
                step(k, k % 2)

            act.wait_ge(s["merge"], MERGE_MAX)
            nmost, zsum = small[:, 12, 2:3], small[:, 12, 4:5]
            act.activation(expo[:], best_of, ACT.Exp, bias=nmost, accum_out=zsum).then_inc(s["exp_done"], 1)
            act.wait_ge(s["merge"], MERGE_PLACE)
            act.activation(vals8[:], vals8[:], ACT.Exp, bias=nmost).then_inc(s["exp_done"], 1)
            act.wait_ge(s["merge"], MERGE_TABLE)
            act.dma_start(table.rearrange("(e c) w -> e c w", e=E), tab[:].rearrange("p l c w -> p (l c) w")
                          ).then_inc(s["table_stored"], 16)
            act.preload_act_table(ACT.Gelu)

            def expert(it, i):
                e = W * it + i
                for m in range(NM):
                    act.wait_ge(s["h_ps"], 2 * e + m // 4 + 1)
                    if m == 0 and past(e, 2):
                        act.wait_ge(s["y2_ps"], e - 1)
                    act.activation(hT[:, i % 2, m, :], h_psum[i % 2][:, m, :], ACT.Gelu,
                                   bias=b1T[:].rearrange("p n c -> p (n c)")[:, one(NM * e + m, 1)]
                                   ).then_inc(s["h_act"], 1)
            for i in range(W):
                expert(0, i)
            with act.Fori(1, LOOPS) as it:
                for i in range(W):
                    expert(it, i)
            act.wait_ge(s["table_stored"], 16)

        @block.tensor
        def _(pe):
            pe.wait_ge(s["ctx_in"], 16)
            pe.wait_ge(s["consts"], C_SHIFTED)
            for c in range(KC):
                for b in range(B):
                    mm = pe.transpose(score_ps[:, c, b * NK:(b + 1) * NK], ctx_sb[:, b, c * P:(c + 1) * P],
                                      ident[0:NK, 0:NK])
            mm.then_inc(s["p_prep"], 1)
            pe.wait_ge(s["v_prep"], V_CTX)
            pe.wait_ge(s["wts_in"], 64)
            for c in range(KC):
                for k in range(KC):
                    mm = pe.matmul(score_ps[:, 2 + c, 0:B * NK], wk[:, k, c * P:(c + 1) * P], ctxT[:, k, :],
                                   start=(k == 0), stop=(k == KC - 1))
            mm.then_inc(s["p_prep"], 1)
            for b in range(B):
                for k in range(KC):
                    mm = pe.matmul(bank[b][0:NK, 0:D], ctxT[:, k, b * NK:(b + 1) * NK], wv[:, k, :],
                                   start=(k == 0), stop=(k == KC - 1))
            mm.then_inc(s["p_prep"], 1)
            pe.wait_ge(s["v_prep"], V_VALUES)
            pe.wait_ge(s["a_prep"], A_KEYS)
            for q in range(KC * NCH):
                a, n, h0, nh = chunk(q % NCH)
                for h in range(nh):
                    at = CH - (NK * (h0 + h) - a)
                    mm = pe.matmul(block_ps(q)[:, :, h * DV:(h + 1) * DV], shifted[:, at:at + n],
                                   vaug[:, :, HH * (q // NCH) + h0 + h, :], start=True, stop=True)
            mm.then_inc(s["p_prep"], 1)
            pe.wait_ge(s["small_in"], 16 * 6)
            for c in range(KC):
                pe.transpose(bank[2][:, c * E:(c + 1) * E], wr_sb[:, c * P:(c + 1) * P], ident[0:E, 0:E])
            for c in range(2):
                for a in range(2):
                    mm = pe.transpose(bank[3][:, (2 * c + a) * 2 * E:(2 * c + a + 1) * 2 * E], b1_sb[:, a, c::2],
                                      ident[0:2 * E, 0:2 * E])
            mm.then_inc(s["p_prep"], 1)
            pe.wait_ge(s["v_prep"], V_PARAMS)
            pe.wait_ge(s["consts"], C_ALL)

            def turn(dst, src, v, done):
                for c in range(KC):
                    mm = pe.transpose(dst[:, c * P:(c + 1) * P], src[:, v, c * P:(c + 1) * P], ident[:])
                mm.then_inc(s[done], 1)

            def turn_probs(k, u, g):
                t, v = k - DLAG, (u + DLAG) % 2
                if g == 0:
                    pe.wait_ge(s["p_exp"], t + 1)
                    if past(t, 1):
                        pe.wait_ge(s["pt_sb"], 3 * t)
                elif g == 2:
                    pe.wait_ge(s["pt_sb"], 3 * t + 1)
                q0, q1 = GROUPS[g]
                for q in range(q0, q1):
                    a, n, _, _ = chunk(q % NCH)
                    a += FLAT * (q // NCH)
                    mm = pe.transpose(bank[g % 2][0:n, (q - q0) * P:(q - q0 + 1) * P], prob[:, v, a:a + n], ident[:])
                mm.then_inc(s["pt_ps"], 1)

            def step(k, u):
                if there(k, SLAG):
                    t, v = k - SLAG, (u + SLAG) % 2
                    pe.wait_ge(s["q_sb"], t + 1)
                    if past(t, 1):
                        pe.wait_ge(s["s_sub"], 2 * t)
                    other = (t // 2 % 4 + 3) // 4 if v == 0 else 1
                    for q, pieces in enumerate(PIECES):
                        first, n = BANKS[q][0], (BANKS[q][1] - BANKS[q][0]) * NK
                        for i, (h0, h1) in enumerate(pieces):
                            c = h0 // HH
                            pe.matmul(score_ps[:, q, (h0 - first) * NK:(h1 - first) * NK], qT[:, v, c, :],
                                      kblk[:, one(t // 8 * KC + c, 1), (h0 - c * HH) * NK:(h1 - c * HH) * NK],
                                      start=(i == 0), stop=False, skip_group_check=True)
                        mm = pe.matmul(score_ps[:, q, 0:n], ident16[:],
                                       bias_tab[:, one(t // 8 * 2 + other, 1), :].broadcast_to([P, n // NK, NK]),
                                       start=False, stop=True, skip_group_check=True)
                    mm.then_inc(s["s_ps"], 1)
                if there(k, TLAG):
                    t, v = k - TLAG, (u + TLAG) % 2
                    pe.wait_ge(s["xn_ready"], t + 1)
                    if there(k, GLAG + 1):
                        pe.wait_ge(s["x2T_sb"], k - GLAG)
                    turn(xt_ps, xn, v, "xT_ps")
                if there(k, DLAG):
                    turn_probs(k, u, 0)
                    turn_probs(k, u, 1)
                if there(k, TLAG):
                    t, v = k - TLAG, (u + TLAG) % 2
                    pe.wait_ge(s["xT_sb"], t + 1)
                    for c in range(KC):
                        for i in range(KC):
                            mm = pe.matmul(q_psum[:, c * P:(c + 1) * P], wq[:, i, c * P:(c + 1) * P], xT[:, v, i, :],
                                           start=(i == 0), stop=(i == KC - 1))
                    mm.then_inc(s["q_ps"], 1)
                if there(k, DLAG):
                    turn_probs(k, u, 2)
                if there(k, OLAG):
                    t, v = k - OLAG, (u + OLAG) % 2
                    pe.wait_ge(s["o_ready"], t + 1)
                    if past(t, 1):
                        pe.wait_ge(s["x1_ready"], t)
                    turn(ot_ps, o_sb, v, "oT_ps")
                if there(k, DLAG):
                    t, v = k - DLAG, (u + DLAG) % 2
                    pe.wait_ge(s["pt_sb"], 3 * t + 3)
                    if past(t, 1):
                        pe.wait_ge(s["o_ready"], t)
                    if there(k, GLAG + 1):
                        pe.wait_ge(s["lg_sb"], k - GLAG)
                    for q in range(KC * NCH):
                        _, n, h0, nh = chunk(q % NCH)
                        h0 += HH * (q // NCH)
                        mm = pe.matmul(pv_psum[:, h0 * DV:(h0 + nh) * DV], probT[0:n, v, q, :],
                                       vblk[0:n, one(t // 8, 1), q, 0:nh * DV],
                                       start=(q == 0), stop=(q == KC * NCH - 1), skip_group_check=True)
                    mm.then_inc(s["pv_ps"], 1)
                if there(k, GLAG):
                    t, v = k - GLAG, (u + GLAG) % 2
                    pe.wait_ge(s["x2_ready"], t + 1)
                    if there(k, TLAG):
                        pe.wait_ge(s["q_sb"], k)
                    turn(xt_ps, x2, v, "x2T_ps")
                if there(k, OLAG):
                    t, v = k - OLAG, (u + OLAG) % 2
                    pe.wait_ge(s["oT_sb"], t + 1)
                    for i in range(KC):
                        mm = pe.matmul(y_psum, oT[:, v, i, :], wo[:, i, :], start=(i == 0), stop=(i == KC - 1))
                    mm.then_inc(s["y_ps"], 1)
                if there(k, GLAG):
                    t, v = k - GLAG, (u + GLAG) % 2
                    pe.wait_ge(s["x2T_sb"], t + 1)
                    if past(t, 1):
                        pe.wait_ge(s["lg_sb"], t)
                    if there(k, DLAG):
                        pe.wait_ge(s["o_ready"], k - DLAG + 1)
                    for i in range(KC):
                        mm = pe.matmul(lg_psum[G2 * v:G2 * v + E, :], wrT[:, i, :], x2T[:, v, i, :],
                                       start=(i == 0), stop=(i == KC - 1))
                    mm.then_inc(s["lg_ps"], 1)
            for k in range(2 * FIRST_PAIR):
                step(k, k % 2)
            with pe.Fori(FIRST_PAIR, LAST_PAIR) as n:
                for u in range(2):
                    step(2 * n + u, u)
            for k in range(NT, NT + GLAG):
                step(k, k % 2)

            pe.wait_ge(s["merge"], MERGE_PLACE)
            pe.transpose(bank[0][:, 0:E], place_of, ident[0:E, 0:E]).then_inc(s["turn"], 1)

            def turn_tokens(e, uses, i):
                pe.wait_ge(xg_in[i % 4], 16 * uses + 16)
                if past(e, 2):
                    pe.wait_ge(s["xg_sb"], e - 1)
                for c in range(KC):
                    mm = pe.transpose(bank[2][:, D * (i % 2) + c * P:D * (i % 2) + (c + 1) * P], xg[i % 4][:, c::2],
                                      ident[:])
                mm.then_inc(s["xg_ps"], 1)

            def hidden(it, i, half):
                e, v = W * it + i, i % 2
                if half == 0:
                    pe.wait_ge(s["xg_sb"], e + 1)
                    pe.wait_ge(w_in[i], 48 * it + 48)
                    if past(e, 2):
                        pe.wait_ge(s["h_act"], NM * (e - 1))
                for m in range(NM // 2 * half, NM // 2 * (half + 1)):
                    sl, c = divmod(m, 2)
                    for k in range(KC):
                        mm = pe.matmul(h_psum[v][:, m, :], w1[i][:, sl, k, c::2], xgT[:, v, k, :],
                                       start=(k == 0), stop=(k == KC - 1))
                mm.then_inc(s["h_ps"], 1)

            def output(e, i):
                v = i % 2
                if past(e, 2):
                    pe.wait_ge(s["yb_done"], e - 1)
                pe.wait_ge(s["h_act"], NM * e + NM)
                for m in range(NM):
                    sl, c = divmod(m, 2)
                    mm = pe.matmul(bank[3 - 2 * v][:, KO * sl:KO * (sl + 1)], hT[:, v, m, :],
                                   w2[i][:, sl, c, :], start=(c == 0), stop=(c == 1))
                mm.then_inc(s["y2_ps"], 1)

            def expert(it, i, last):
                e = W * it + i
                hidden(it, i, 0)
                if past(e, 1):
                    output(e - 1, (i - 1) % W)
                if not last or i + 1 < W:
                    turn_tokens(e + 1, 2 * it + (i + 1) // 4, i + 1)
                hidden(it, i, 1)
            turn_tokens(0, 0, 0)
            for i in range(W):
                expert(0, i, False)
            with pe.Fori(1, LOOPS - 1) as it:
                for i in range(W):
                    expert(it, i, False)
            for i in range(W):
                expert(LOOPS - 1, i, True)
            output(E - 1, W - 1)


_INS = ["x", "ctx_1024", "mask_BxS2_if1", "g_xattn", "g_ffn", "L0_xattn_Wq", "L0_xattn_Wk", "L0_xattn_Wv",
        "L0_xattn_Wo", "L0_ffn_Wr", "L0_ffn_W1", "L0_ffn_b1", "L0_ffn_W2", "L0_ffn_b2"]


def kernel(**inputs):
    import numpy as _np
    import concourse.bacc as _bacc
    from concourse import mybir as _mybir
    from concourse.bass_utils import run_bass_kernel_spmd as _run

    nc = _bacc.Bacc("TRN2", target_bir_lowering=False, num_devices=1)
    arrays, args = {}, []
    for name in _INS:
        a = _np.ascontiguousarray(inputs[name])
        arrays[f"in_{name}_dram"] = a
        args.append(nc.dram_tensor(f"in_{name}_dram", a.shape, _mybir.dt.from_np(a.dtype), kind="ExternalInput").ap())
    args.append(nc.dram_tensor("out_0_dram", (B, N, D), F32, kind="ExternalOutput").ap())
    build(nc, *args)
    r = _run(nc, [arrays], core_ids=[0])
    return r.results[0]["out_0_dram"]
```

```python
from contextlib import ExitStack

import concourse.bass as bass
from concourse import mybir

F32 = mybir.dt.float32
BF16 = mybir.dt.bfloat16
I32 = mybir.dt.int32
U32 = mybir.dt.uint32
ALU = mybir.AluOpType
ACT = mybir.ActivationFunctionType
AX = mybir.AxisListType
one = bass.ds

P = 128
B, N, D = 4, 1024, 256
NK = 77
H, DK = 16, 16
DV = DK + 1
E, S, M, KO = 48, 4, 256, 64
KC = D // P
TOK = B * N
NT = TOK // P
CAP = int(1.5 * TOK / E)
EPS = 1e-5
HH = H // KC
FLAT = HH * NK
BANKS = ((0, 4), (4, 10), (10, 16))
CH = 124
NCH = -(-FLAT // CH)
HALF = N // 2
G2 = 64
LP = G2 + E
LT = 4
GT = LT // 2
NG = NT // LT
NL = 2 * NG
GB = NG // B
SORT = CAP.bit_length() - 1
ROUNDS = CAP // 8
RS = ROUNDS // LT
STEPS = NG * LT
W = 8
LOOPS = E // W
NM = S * 2
MASKED = -1e30
TAKEN = -3e38
GROUPS = ((0, 4), (4, 8), (8, 10))
PIECES = (((0, 4),), ((4, 8), (8, 10)), ((10, 16),))
FEW, MANY = 4, 6
TLAG, SLAG, DLAG, OLAG, GLAG = 1, 2, 3, 4, 5
FIRST_PAIR, LAST_PAIR = 4, NT // 2
SETS = NT // 8
PICK = GLAG + LT
META = 6
AHEAD = 3

V_CTX = 1 + KC
V_BIAS = V_CTX + HH + 2
V_VALUES = V_BIAS + B + 2 * B
V_BLOCKS = V_VALUES + KC * NCH
V_PARAMS = V_BLOCKS + 2
C_IDENT, C_SHIFTED, C_HEADS, C_ALL = 2, 4, 7, 14
C_MERGE = C_ALL + 16
A_GATE = 1
A_KEYS = A_GATE + HH
MERGE_LIM, MERGE_PLACE, MERGE_SUM = 21, 49, 52


def chunk(i):
    a = CH * i
    n = min(CH, FLAT - a)
    return a, n, a // NK, (a + n - 1) // NK - a // NK + 1


def there(k, lag):
    return not isinstance(k, int) or 0 <= k - lag < NT


def past(t, back):
    return not isinstance(t, int) or t >= back


def stat_tiles(k):
    return [k] + [8 + (SETS - 1) * k + i for i in range(SETS - 1)] if k < 8 else []


def apart(eng, s, value):
    value = value if isinstance(value, int) else eng.to_reg(value)
    eng.wait_ge(s["ready"], 1)
    return value


def sort_stage(dve, a, b, n, w):
    av, bv = (t[:, 0:n * CAP].rearrange("p (m t w) -> p m t w", t=2, w=w) for t in (a, b))
    return (dve.tensor_tensor(bv[:, :, 0, :], av[:, :, 0, :], av[:, :, 1, :], ALU.max),
            dve.tensor_tensor(bv[:, :, 1, :], av[:, :, 0, :], av[:, :, 1, :], ALU.min))


def build(nc, x, ctx_in, mask, g_xattn, g_ffn, Wq, Wk, Wv, Wo, Wr, W1, b1, W2, b2, out):
    normed = nc.dram_tensor("normed", [TOK, D], F32, kind="Internal").ap()
    table = nc.dram_tensor("table", [E * NL * CAP, 2], F32, kind="Internal").ap()
    out_rows = out.rearrange("b n d -> (b n) d")
    with ExitStack() as ctx:
        def sb(name, shape, dt=F32):
            return ctx.enter_context(nc.sbuf_tensor(name, shape, dt))

        score_ps = ctx.enter_context(nc.psum_tensor("score_ps", [P, 4, 512], F32))
        bank = [ctx.enter_context(nc.psum_tensor(f"bank{i}", [P, 512], F32)) for i in range(4)]
        names = """ready ctx_in wts_in small_in consts v_prep a_prep p_prep
            stat1 aggr1 var1 rstd1 xn_ready xT_ps xT_sb q_ps q_sb s_ps top_done s_sub p_exp pt_ps pt_sb pv_ps den_done
            o_ready oT_ps oT_sb y_ps x1_ready stat2 aggr2 var2 rstd2 x2_ready x2T_ps x2T_sb lg_ps lg_sb
            loaded eight places taken filed out_stored premerge ids_done merge exp_done turn table_stored slots_ready
            picked xg_ps xg_sb h_ps h_act y2_ps yb_done yo_ready scattered""".split()
        s = {n: ctx.enter_context(nc.semaphore(n)) for n in names}
        x_in = [ctx.enter_context(nc.semaphore(f"x_in{i}")) for i in range(2 * B)]
        x2_stored = [ctx.enter_context(nc.semaphore(f"x2_stored{i}")) for i in range(2)]
        w_in = [ctx.enter_context(nc.semaphore(f"w_in{i}")) for i in range(W)]
        meta_in = [ctx.enter_context(nc.semaphore(f"meta_in{i}")) for i in range(W)]
        xg_in = [ctx.enter_context(nc.semaphore(f"xg_in{i}")) for i in range(4)]

        xall = sb("xall", [P, NT, D])
        wq, wk, wv, wo = (sb(n, [P, KC, D]) for n in ("wq", "wk", "wv", "wo"))
        kblk = sb("kblk", [P, B * KC, FLAT])
        vblk = sb("vblk", [CH, B, KC * NCH, 3 * DV])
        wrT = sb("wrT", [P, KC, E])
        b1T = sb("b1T", [P, E * S, 2])
        mask_col = sb("mask_col", [NK, B], I32)
        keep_col = sb("keep_col", [NK, B])
        bias_tab = sb("bias_tab", [P, 2 * B, NK], BF16)
        ident = sb("ident", [P, P])
        ident16 = sb("ident16", [P, P], BF16)
        head_of = sb("head_of", [P, HH])
        minus_half = sb("minus_half", [P, 1])
        gate_in = sb("gate_in", [P, 2])
        filler = sb("filler", [1, 4])
        gate = sb("gate", [P, 2])
        xn = sb("xn", [P, 2, D])
        xT = sb("xT", [P, 2, KC, P])
        qT = sb("qT", [P, 2, KC, P])
        prob = sb("prob", [P, 2, H * NK])
        probT = sb("probT", [P, 2, KC * NCH, P])
        early_t, early_p = probT[:].rearrange("p a q t -> p (a q t)"), prob[:].rearrange("p a f -> p (a f)")
        ctx_sb = early_t[0:NK, 0:B * D].rearrange("p (b d) -> p b d", b=B)
        ctxT = early_t[:, B * D:B * D + KC * B * NK].rearrange("p (c n) -> p c n", c=KC)
        vaug = early_p[0:NK, 0:B * H * DV].rearrange("p (b h d) -> p b h d", b=B, h=H)
        b1_sb = early_p[0:2 * E, B * H * DV:B * H * DV + 2 * M].rearrange("p (a m) -> p a m", a=2)
        wr_sb = early_p[0:E, B * H * DV + 2 * M:B * H * DV + 2 * M + D]
        shifted = early_p[0:NK, B * H * DV + 2 * M + D:B * H * DV + 2 * M + D + 2 * CH + NK]
        after = B * D + KC * B * NK
        row_bias, mask_f = (early_t[:, after + i * B * NK:after + (i + 1) * B * NK].rearrange("p (b k) -> p b k", b=B)
                            for i in range(2))
        mask_row = mask_f.bitcast(I32)
        top = sb("top", [P, 2, H])
        den = sb("den", [P, 2, H])
        o_sb = sb("o_sb", [P, 2, D])
        oT = sb("oT", [P, 2, KC, P])
        x2 = sb("x2", [P, 2, D])
        x2T = sb("x2T", [P, 2, KC, P])
        ln1 = [sb(f"ln1_{n}", [P, *w]) for n, w in (("st", (SETS, 6)), ("mv", (NT, 2)), ("var", (NT, 1)),
                                                    ("rstd", (NT, 2)))]
        ln2 = [sb(f"ln2_{n}", [P, 2, w]) for n, w in (("st", 6), ("mv", 2), ("var", 1), ("rstd", 2))]
        logit = sb("logit", [LP, GB * GT * P])
        work = sb("work", [LP, GT * P])
        m8 = sb("m8", [LP, 2, RS, 8])
        i8 = sb("i8", [LP, 2, RS, 8], U32)
        lval = sb("lval", [LP, NG, CAP])
        lidx = sb("lidx", [LP, NG, CAP], BF16)
        logit_by_group = logit[:].rearrange("p (h c) -> p h c", h=GB)
        lval_by_step, lidx_by_step = (a[:].rearrange("p g (s w) -> p (g s) w", s=LT) for a in (lval, lidx))
        w1 = [sb(f"w1_{i}", [P, S, KC, M]) for i in range(W)]
        w2 = [sb(f"w2_{i}", [P, S, 2, KO]) for i in range(W)]
        b2r = [sb(f"b2r_{i}", [P, D]) for i in range(W)]
        slot_of = sb("slot_of", [P, E], U32)
        pick = sb("pick", [P, W], U32)
        meta = sb("meta", [P, W, 2])
        hT = probT[:, :, 0:NM, :]
        xg = [xn[:, 0, :], xn[:, 1, :]] + [qT[:, a].rearrange("p c t -> p (c t)") for a in range(2)]
        xgT, yb, yo = xT, o_sb, x2
        listbase_i = sb("listbase_i", [LP, NG], I32)
        listbase = sb("listbase", [LP, NG])
        slot_i = lval[:, 0, :].bitcast(I32)
        base_i = lval[:, 1, :].bitcast(I32)
        slot_f = sb("slot_f", [LP, CAP])
        base_f = sb("base_f", [LP, CAP])
        both = sb("both", [LP, E])
        lim = sb("lim", [LP, 2])
        wz = sb("wz", [LP, 2])
        counts = sb("counts", [LP, 2, NG])
        cuts = sb("cuts", [LP, 2, NG])
        cnt = sb("cnt", [E, 2, NL])
        cut = sb("cut", [E, 2, NL])
        run = sb("run", [E, 4, NG + NL])
        small = sb("small", [E, 3, NL])
        need, avail, eq = small[:, 0, 0:1], small[:, 1, :], small[:, 2, :]
        free = kblk[0:LP].rearrange("p a f -> p (a f)")
        at = [0]

        def take(n):
            at[0] += n
            return free[:, at[0] - n:at[0]]
        above, at_least, vexp = (take(NG * CAP).rearrange("p (l c) -> p l c", l=NG) for _ in range(3))
        ahead_a, ahead_b = take(3 * CAP), take(3 * CAP)
        sort_a, sort_b = take(CAP), take(CAP)
        lower, expo, place = take(CAP)[0:E], take(CAP)[0:E], take(CAP)
        best = sort_a[0:E]
        ids_f = probT[0:LP].rearrange("p a q t -> p (a q t)")[:, 0:NG * CAP].rearrange("p (l c) -> p l c", l=NG)
        tab = prob[0:LP].rearrange("p a f -> p (a f)")[:, 0:NG * CAP * 2].rearrange("p (l c w) -> p l c w", l=NG, w=2)
        xpairs = xall[:].rearrange("p (n u) d -> p n u d", u=2)
        xt_ps, q_psum = bank[2][:, 0:D], bank[2][:, D:2 * D]
        ot_ps, y_psum = bank[3][:, 0:D], bank[3][:, D:2 * D]
        pv_psum, lg_psum = score_ps[:, 3, 0:H * DV], score_ps[:, 0, 512 - P:]
        h_psum = [score_ps[:, 2 * v:2 * v + 2, :].rearrange("p a (m t) -> p (a m) t", t=P) for v in range(2)]

        def block_ps(q):
            c, i = divmod(q, NCH)
            _, n, _, nh = chunk(i)
            starts = [0, 0]
            for m in range(i):
                starts[m // 3] += B * DV * chunk(m)[3]
            a = starts[i // 3]
            return score_ps[0:n, 2 * c + i // 3, a:a + B * DV * nh].rearrange("p (b w) -> p b w", b=B)

        block = ctx.enter_context(nc.Block())

        @block.sync
        def _(sp):
            def load_x(b, u):
                sp.dma_start(xpairs[:, 4 * b:4 * b + 4, u, :],
                             x[b, u * HALF:(u + 1) * HALF, :].rearrange("(j p) d -> p j d", p=P)
                             ).then_inc(x_in[2 * b + u], 16)

            def load_weights(e, i):
                sp.dma_start(w1[i][:], W1[one(e, 1)][0].rearrange("s (p c) m -> p s c m", c=KC)).then_inc(w_in[i], 16)
                sp.dma_start(w2[i][:], W2[one(e, 1)][0].rearrange("s (p c) k -> p s c k", c=2)).then_inc(w_in[i], 16)
                sp.dma_start(b2r[i][:], b2[one(e, 1)].rearrange("a s k -> a (s k)").broadcast_to([P, D])
                             ).then_inc(w_in[i], 16)

            def store_normed(b, j, u):
                sp.wait_ge(s["x2_ready"], 8 * b + 2 * j + u + 1)
                sp.dma_start(normed[one((8 * b + j + 4 * u) * P, P)], x2[:, u, :]).then_inc(x2_stored[u], 16)

            sp.dma_start(ctx_sb, ctx_in.rearrange("b k d -> k b d")).then_inc(s["ctx_in"], 16)
            load_x(0, 0)
            for dst, src in ((wk, Wk), (wv, Wv), (wq, Wq), (wo, Wo)):
                sp.dma_start(dst[:], src.rearrange("(k p) n -> p k n", p=P)).then_inc(s["wts_in"], 16)
            for i in range(1, 2 * B):
                load_x(i // 2, i % 2)
            for i in range(W):
                load_weights(i, i)
            with sp.Fori(0, B) as b:
                with sp.Fori(0, 4) as j:
                    store_normed(b, j, 0)
                    store_normed(b, j, 1)
                for u in range(2):
                    sp.dma_start(out[one(b, 1)][0][u * HALF:(u + 1) * HALF].rearrange("(j p) d -> p j d", p=P),
                                 xpairs[:, one(4 * b, 4), u, :]).then_inc(s["out_stored"], 16)
            with sp.Fori(1, LOOPS) as it:
                for i in range(W):
                    sp.wait_ge(s["y2_ps"], W * it + i - W + 1)
                    sp.wait_ge(s["yb_done"], W * it + i - W + 1)
                    load_weights(W * it + i, i)
            sp.wait_ge(s["out_stored"], 16 * 2 * B)

        @block.gpsimd
        def _(pool):
            made = [0]

            def make(ins):
                made[0] += 1
                ins.then_inc(s["consts"], 1)
                pool.wait_ge(s["consts"], made[0])

            def affine(t, compare, fill, base, pattern, channel):
                make(pool.affine_select(out=t, in_=t, compare_op=compare, fill=fill, base=base, pattern=pattern,
                                        channel_multiplier=channel))
            make(pool.memset(ident[:], 0.0))
            affine(ident[:], ALU.not_equal, 1.0, 0, [[-1, P]], 1)
            make(pool.memset(shifted, 0.0))
            affine(shifted, ALU.not_equal, 1.0, CH, [[-1, 2 * CH + NK]], 1)
            make(pool.memset(head_of[:], 1.0))
            affine(head_of[:], ALU.is_ge, 0.0, 0, [[-DK, HH]], 1)
            affine(head_of[:], ALU.is_ge, 0.0, DK - 1, [[DK, HH]], -1)
            make(pool.memset(minus_half[:], -0.5))
            make(pool.memset(logit[:], 0.0))
            for i, (n, by) in enumerate((("filed", 4), ("taken", 1), ("loaded", 2), ("ready", 1))):
                pool.memset(filler[:, i:i + 1], 0.0).then_inc(s[n], by)
            make(pool.tensor_copy(ident16[:], ident[:]))
            pool.wait_ge(s["v_prep"], V_BIAS)
            for b in range(B):
                make(pool.affine_select(out=bias_tab[:, 2 * b, :], in_=row_bias[:, b, :], compare_op=ALU.is_ge,
                                        fill=MASKED, base=0, pattern=[[-1, NK]], channel_multiplier=1))
            assert made[0] == C_ALL
            make(pool.iota(listbase_i[:], pattern=[[N, B], [GT * P, GB]], base=0, channel_multiplier=0))
            make(pool.iota(listbase_i[G2:LP], pattern=[[N, B], [GT * P, GB]], base=HALF, channel_multiplier=0))
            make(pool.iota(slot_i, pattern=[[1, CAP]], base=0, channel_multiplier=0))
            make(pool.memset(base_f[:], 0.0))
            make(pool.iota(base_i, pattern=[[1, CAP]], base=0, channel_multiplier=NL * CAP))
            make(pool.tensor_copy(listbase[:], listbase_i[:]))
            make(pool.tensor_copy(slot_f[:], slot_i))
            make(pool.tensor_copy(base_f[0:E], base_i[0:E]))
            for t in (both, lim, wz, counts, cuts, run):
                make(pool.memset(t[:], 0.0))
            make(pool.tensor_copy(both[0:E], ident[0:E, 0:E]))
            make(pool.tensor_copy(both[G2:LP], ident[0:E, 0:E]))
            assert made[0] == C_MERGE

            def rstd(n, i, ln, ready, mid, done):
                _, mv, var, to = ln
                pool.wait_ge(s[ready], apart(pool, s, n + 1))
                pool.tensor_scalar(var[:, i, :], mv[:, i, 1:2], EPS, None, ALU.add).then_inc(s[mid], 1)
                pool.wait_ge(s[mid], 2 * n + 1)
                pool.tensor_tensor(to[:, i, 0:1], var[:, i, :], minus_half[:], ALU.pow).then_inc(s[mid], 1)
                pool.wait_ge(s[mid], apart(pool, s, 2 * n + 2))
                pool.tensor_scalar(to[:, i, 1:2], mv[:, i, 0:1], to[:, i, 0:1], -1.0, ALU.mult, ALU.mult
                                   ).then_inc(s[done], 1)

            def file(q, v):
                pool.wait_ge(s["places"], RS * q + RS)
                pool.tensor_copy(lval_by_step[:, one(q, 1), :], m8[:, v:v + 1].rearrange("p a r w -> p a (r w)")
                                 ).then_inc(s["filed"], 1)
                pool.tensor_copy(lidx_by_step[:, one(q, 1), :], i8[:, v:v + 1].rearrange("p a r w -> p a (r w)")
                                 ).then_inc(s["filed"], 1)

            def step(k, u):
                tiles = stat_tiles(k) if isinstance(k, int) else []
                for i, t in enumerate(tiles[0:1]):
                    rstd(SETS * k + i, t, ln1, "aggr1", "var1", "rstd1")
                if past(k, PICK + 1):
                    file(k - PICK - 1, (u + PICK + 1) % 2)
                if there(k, OLAG):
                    rstd(k - OLAG, (u + OLAG) % 2, ln2, "aggr2", "var2", "rstd2")
                for i, t in enumerate(tiles[1:], 1):
                    rstd(SETS * k + i, t, ln1, "aggr1", "var1", "rstd1")

            for k in range(PICK + 1):
                step(k, k % 2)
            with pool.Fori((PICK + 1) // 2, LAST_PAIR) as n:
                for u in range(2):
                    step(2 * n + u, u)
            for k in range(NT, NT + GLAG):
                step(k, k % 2)
            q = NT + GLAG - PICK - 1
            file(q, q % 2)
            assert q + 1 == STEPS - LT

            for q in range(STEPS - LT, STEPS):
                file(q, q % 2)
            pool.wait_ge(s["filed"], 2 * STEPS + 4)
            pool.tensor_tensor(ids_f, lidx[:], listbase[:].rearrange("p (l a) -> p l a", a=1)
                               .broadcast_to([LP, NG, CAP]), ALU.add).then_inc(s["ids_done"], 1)
            pool.wait_ge(s["ids_done"], 1)
            pool.tensor_copy(tab[:, :, :, 0].bitcast(U32), ids_f).then_inc(s["ids_done"], 1)

            def gather_meta(e, i):
                pool.tensor_copy(pick[:, i:i + 1], slot_of[:, one(e, 1)]).then_inc(s["picked"], 1)
                pool.wait_ge(s["picked"], apart(pool, s, e + 1))
                pool.indirect_dma_start(meta[:, i, :], None, table,
                                        bass.IndirectOffsetOnAxis(ap=pick[:, i:i + 1], axis=0)
                                        ).then_inc(meta_in[i], 16)

            def gather_tokens(e, uses, i):
                pool.wait_ge(meta_in[i], apart(pool, s, 16 * uses + 16))
                if past(e, 4):
                    pool.wait_ge(s["xg_ps"], apart(pool, s, e - 3))
                pool.indirect_dma_start(xg[i % 4], None, normed,
                                        bass.IndirectOffsetOnAxis(ap=meta[:, i, 0:1].bitcast(U32), axis=0)
                                        ).then_inc(xg_in[i % 4], 16)

            def scatter(e, i):
                pool.wait_ge(s["yo_ready"], apart(pool, s, e + 1))
                if past(e, 1):
                    pool.wait_ge(s["scattered"], apart(pool, s, 16 * e))
                pool.indirect_dma_start(out_rows, bass.IndirectOffsetOnAxis(ap=meta[:, i, 0:1].bitcast(U32), axis=0),
                                        yo[:, i % 2, :], None, compute_op=ALU.add).then_inc(s["scattered"], 16)

            def expert(it, i, last):
                e = W * it + i
                if not last or i + AHEAD < W:
                    gather_tokens(e + AHEAD, it + (i + AHEAD) // W, (i + AHEAD) % W)
                scatter(e, i)
                if not last or i + META < W:
                    gather_meta(e + META, (i + META) % W)

            pool.wait_ge(s["slots_ready"], 1)
            pool.wait_ge(s["table_stored"], 32)
            for u in range(2):
                pool.wait_ge(x2_stored[u], 16 * NT // 2)
            pool.wait_ge(s["out_stored"], 16 * 2 * B)
            for e in range(AHEAD):
                gather_meta(e, e)
            for e in range(AHEAD):
                gather_tokens(e, 0, e)
            for e in range(AHEAD, META):
                gather_meta(e, e)
            for i in range(W):
                expert(0, i, False)
            with pool.Fori(1, LOOPS - 1) as it:
                for i in range(W):
                    expert(it, i, False)
            for i in range(W):
                expert(LOOPS - 1, i, True)
            pool.wait_ge(s["scattered"], 16 * E)

        @block.vector
        def _(dve):
            prep = [0]

            def link(ins):
                prep[0] += 1
                ins.then_inc(s["v_prep"], 1)
                dve.wait_ge(s["v_prep"], prep[0])
            link(dve.memset(bank[1][:], 0.0))
            dve.wait_ge(s["p_prep"], 1)
            for c in range(KC):
                link(dve.tensor_copy(ctxT[:, c, :], score_ps[:, c, 0:B * NK]))
            assert prep[0] == V_CTX
            dve.wait_ge(s["p_prep"], 2)
            dve.wait_ge(s["consts"], C_HEADS)
            keys = kblk[:].rearrange("p (b c) (h k) -> p b c h k", c=KC, h=HH)
            for h in range(HH):
                link(dve.tensor_scalar(keys[:, :, 0, h, :], score_ps[:, 2, 0:B * NK].rearrange("p (b k) -> p b k", b=B),
                                       head_of[:, h:h + 1], None, ALU.mult))
            dve.wait_ge(s["small_in"], 16 * 6)
            link(dve.tensor_scalar(keep_col[:], mask_col[:], 0.0, None, ALU.not_equal))
            link(dve.tensor_scalar(row_bias, mask_row, 0.0, MASKED, ALU.is_equal, ALU.mult))
            assert prep[0] == V_BIAS
            for b in range(B):
                link(dve.tensor_copy(bias_tab[:, 2 * b + 1, :], row_bias[:, b, :]))
            dve.wait_ge(s["p_prep"], 3)
            for b in range(B):
                link(dve.tensor_scalar(vaug[:, b, :, 0:DK], bank[b][0:NK, 0:D].rearrange("p (h d) -> p h d", h=H),
                                       keep_col[:, b:b + 1], None, ALU.mult))
                link(dve.tensor_copy(vaug[:, b, :, DK:DV],
                                     keep_col[:, b:b + 1].broadcast_to([NK, H])))
            assert prep[0] == V_VALUES

            def prepare_rest():
                for c in range(KC):
                    dve.wait_ge(s["p_prep"], 4 + c)
                    for q in range(NCH * c, NCH * (c + 1)):
                        _, n, _, nh = chunk(q % NCH)
                        link(dve.tensor_copy(vblk[0:n, :, q, 0:nh * DV], block_ps(q)))
                assert prep[0] == V_BLOCKS
                dve.wait_ge(s["p_prep"], 6)
                link(dve.tensor_copy(wrT[:], bank[0][:, 0:KC * E].rearrange("p (c e) -> p c e", c=KC)))
                link(dve.tensor_copy(b1T[:].rearrange("p n c -> p c n"),
                                     bank[1][:, 0:2 * E * S].rearrange("p (c n) -> p c n", c=2)))
                assert prep[0] == V_PARAMS
                dve.wait_ge(s["a_prep"], A_GATE)

            def load_logits(g):
                dve.wait_ge(s["lg_sb"], LT * g + LT)
                dve.wait_ge(s["taken"], ROUNDS * g + 1)
                dve.tensor_copy(work[:].rearrange("p (a c) -> p a c", a=1), logit_by_group[:, one(g % GB, 1), :]
                                ).then_inc(s["loaded"], 1)

            def most_of(q, v, rr, first=False):
                if first:
                    dve.wait_ge(s["loaded"], apart(dve, s, q // LT + 3))
                else:
                    dve.wait_ge(s["taken"], apart(dve, s, RS * q + rr + 1))
                if rr == 0:
                    dve.wait_ge(s["filed"], apart(dve, s, 2 * q + 2))
                dve.max(m8[:, v, rr, :], work[:]).then_inc(s["eight"], 1)

            def places_of(q, v, rr):
                dve.wait_ge(s["eight"], apart(dve, s, RS * q + rr + 1))
                dve.max_index(i8[:, v, rr, :], m8[:, v, rr, :], work[:]).then_inc(s["places"], 1)

            def take_out(q, v, rr):
                dve.wait_ge(s["places"], apart(dve, s, RS * q + rr + 1))
                dve.match_replace(work[:], m8[:, v, rr, :], work[:], TAKEN).then_inc(s["taken"], 1)

            def statistics(k, places):
                for i in places:
                    if k:
                        dve.wait_ge(s["aggr1"], SETS * (k - 1) + i + 1)
                    dve.bn_stats(ln1[0][:, i, :], xall[:, stat_tiles(k)[i], :]).then_inc(s["stat1"], 1)
                for i in places:
                    dve.wait_ge(s["stat1"], SETS * k + i + 1)
                    dve.bn_aggr(ln1[1][:, stat_tiles(k)[i], :], ln1[0][:, i, :]).then_inc(s["aggr1"], 1)

            def step(k, u):
                q, vq = k - PICK, (u + PICK) % 2
                picking = past(k, PICK)
                first = picking and (u - PICK) % LT == 0
                t, v = k - SLAG, (u + SLAG) % 2
                if there(k, SLAG):
                    many = score_ps[:, 1:3, 0:MANY * NK].rearrange("p q (h k) -> p q h k", h=MANY)
                    few = score_ps[:, 0, 0:FEW * NK].rearrange("p (h k) -> p h k", h=FEW)
                    p = prob[:, v, :].rearrange("p (h k) -> p h k", k=NK)
                    dve.wait_ge(s["s_ps"], t + 1)
                    dve.tensor_reduce(top[:, v, FEW:].rearrange("p (q h) -> p q h", q=2), many, AX.X, ALU.max
                                      ).then_inc(s["top_done"], 1)
                if first:
                    load_logits(q // LT)
                if picking:
                    most_of(q, vq, 0, first)
                if there(k, SLAG):
                    dve.tensor_reduce(top[:, v, 0:FEW], few, AX.X, ALU.max).then_inc(s["top_done"], 1)
                if picking:
                    places_of(q, vq, 0)
                if there(k, SLAG):
                    dve.wait_ge(s["top_done"], 2 * t + 2)
                    if past(t, 2):
                        dve.wait_ge(s["pt_ps"], 3 * (t - 1))
                    dve.tensor_tensor(p[:, FEW:, :].rearrange("p (q h) k -> p q h k", q=2), many,
                                      top[:, v, FEW:].rearrange("p (q h a) -> p q h a", q=2, a=1)
                                      .broadcast_to([P, 2, MANY, NK]), ALU.subtract).then_inc(s["s_sub"], 1)
                if picking:
                    take_out(q, vq, 0)
                if there(k, SLAG):
                    dve.tensor_tensor(p[:, 0:FEW, :], few, top[:, v, 0:FEW].rearrange("p (h a) -> p h a", a=1)
                                      .broadcast_to([P, FEW, NK]), ALU.subtract).then_inc(s["s_sub"], 1)
                if picking:
                    most_of(q, vq, 1)
                    places_of(q, vq, 1)
                    take_out(q, vq, 1)
                    most_of(q, vq, 2)
                t, v = k - DLAG, (u + DLAG) % 2
                if there(k, DLAG):
                    pv = pv_psum.rearrange("p (h d) -> p h d", d=DV)
                    inverse = den[:, v, :].rearrange("p (h a) -> p h a", a=1)
                    dve.wait_ge(s["pv_ps"], t + 1)
                    dve.reciprocal(inverse, pv[:, :, DK:DV]).then_inc(s["den_done"], 1)
                if picking:
                    places_of(q, vq, 2)
                if there(k, DLAG):
                    dve.wait_ge(s["den_done"], t + 1)
                    if past(t, 2):
                        dve.wait_ge(s["oT_ps"], t - 1)
                    dve.tensor_tensor(o_sb[:, v, :].rearrange("p (h d) -> p h d", d=DK), pv[:, :, 0:DK],
                                      inverse.broadcast_to([P, H, DK]), ALU.mult).then_inc(s["o_ready"], 1)
                if picking:
                    take_out(q, vq, 2)
                    most_of(q, vq, 3)
                t, v = k - OLAG, (u + OLAG) % 2
                if there(k, OLAG):
                    dve.wait_ge(s["y_ps"], t + 1)
                    dve.scalar_tensor_tensor(out=xall[:, one(t, 1), :], in0=y_psum.rearrange("p (a d) -> p a d", a=1),
                                             scalar=gate[:, 0:1], in1=xall[:, one(t, 1), :], op0=ALU.mult,
                                             op1=ALU.add).then_inc(s["x1_ready"], 1)
                if picking:
                    places_of(q, vq, 3)
                if there(k, OLAG):
                    dve.wait_ge(s["x1_ready"], apart(dve, s, t + 1))
                    dve.bn_stats(ln2[0][:, v, :], xall[:, one(t, 1), :]).then_inc(s["stat2"], 1)
                if picking:
                    take_out(q, vq, 3)
                if there(k, OLAG):
                    dve.wait_ge(s["stat2"], apart(dve, s, t + 1))
                    dve.bn_aggr(ln2[1][:, v, :], ln2[0][:, v, :]).then_inc(s["aggr2"], 1)

            for k in range(3 * LT):
                if k < 8:
                    if k in (0, 2):
                        for i in (range(4), None, range(4, 2 * B))[k]:
                            dve.wait_ge(x_in[i], 16)
                    statistics(k, range(1))
                if k == 2:
                    prepare_rest()
                step(k, k % LT)
                if k < 8:
                    statistics(k, range(1, SETS))
            with dve.Fori(3, NT // LT) as n:
                for u in range(LT):
                    step(LT * n + u, u)
            for k in range(NT, NT + GLAG):
                step(k, k % LT)

            ordered = [0]

            def order_some(i):
                level, stage = divmod(i, SORT + 1)
                if i:
                    dve.wait_ge(s["premerge"], ordered[0])
                a, b = (ahead_a, ahead_b) if stage % 2 else (ahead_b, ahead_a)
                n = (3, 2, 1)[level]
                if stage:
                    ins = sort_stage(dve, a, b, n, CAP >> stage)
                elif level == 0:
                    ins = (dve.tensor_tensor(b[:].rearrange("p (n c) -> p n c", n=n), lval[:, 0:6:2, :],
                                             lval[:, 1:6:2, ::-1], ALU.max),)
                else:
                    ins = (dve.tensor_tensor(b[:, 0:CAP], a[:, 0:CAP], a[:, CAP:2 * CAP][:, ::-1], ALU.max),)
                    if level == 1:
                        ins += (dve.tensor_tensor(b[:, CAP:2 * CAP], a[:, 2 * CAP:3 * CAP], lval[:, 6, ::-1],
                                                  ALU.max),)
                for one_of in ins:
                    one_of.then_inc(s["premerge"], 1)
                ordered[0] += len(ins)
            dve.wait_ge(s["filed"], 2 * (STEPS - LT) + 4)
            for r in range(ROUNDS):
                q, rr = STEPS - LT + r // RS, r % RS
                if r == 0:
                    load_logits(NG - 1)
                most_of(q, q % 2, rr, r == 0)
                if 2 * r < 3 * (SORT + 1):
                    order_some(2 * r)
                places_of(q, q % 2, rr)
                if 2 * r < 3 * (SORT + 1):
                    order_some(2 * r + 1)
                take_out(q, q % 2, rr)

            merged = [0]

            def then(ins, more=False):
                merged[0] += 1
                ins.then_inc(s["merge"], 1)
                if not more:
                    dve.wait_ge(s["merge"], merged[0])
            dve.wait_ge(s["premerge"], ordered[0])
            dve.wait_ge(s["filed"], 2 * STEPS + 4)
            dve.wait_ge(s["consts"], C_MERGE)
            then(dve.tensor_tensor(sort_a, ahead_b[:, 0:CAP], lval[:, NG - 1, ::-1], ALU.max))
            for stage in range(SORT):
                larger, smaller = sort_stage(dve, *((sort_b, sort_a) if stage % 2 else (sort_a, sort_b)), 1,
                                             CAP >> stage + 1)
                then(larger, True)
                then(smaller)
            then(dve.tensor_copy(lower, sort_b[G2:LP]))
            then(dve.tensor_tensor(best, sort_b[0:E], lower[:, ::-1], ALU.max))
            then(dve.tensor_reduce(lim[0:E, 0:1], best, AX.X, ALU.min), True)
            then(dve.tensor_reduce(lim[0:E, 1:2], best, AX.X, ALU.max))
            then(dve.tensor_scalar(lim[0:E, 1:2], lim[0:E, 1:2], -1.0, None, ALU.mult))
            then(dve.tensor_copy(lim[G2:LP], lim[0:E]))
            assert merged[0] == MERGE_LIM, merged[0]
            then(dve.tensor_scalar(above, lval[:], lim[:, 0:1], None, ALU.is_gt), True)
            then(dve.tensor_scalar(at_least, lval[:], lim[:, 0:1], None, ALU.is_ge))
            then(dve.tensor_reduce(counts[:, 0, :], above, AX.X, ALU.add), True)
            then(dve.tensor_reduce(counts[:, 1, :], at_least, AX.X, ALU.add))

            def by_list(t, half):
                return t[:].rearrange("p k (b u h) -> p k b u h", b=B, u=2)[:, :, :, half, :]

            def of_half(t, half):
                return t[G2 * half:G2 * half + E].rearrange("p k (b h) -> p k b h", b=B)
            for half in range(2):
                then(dve.tensor_copy(by_list(cnt, half), of_half(counts, half)), half == 0)
            gt, ge = cnt[:, 0, :], cnt[:, 1, :]

            def sums(a, b, to):
                w = 1
                while w < NL:
                    if 2 * w == NL:
                        dst = to
                    else:
                        dst = run[:, b, NG:]
                    then(dve.tensor_tensor(dst, run[:, a, NG:], run[:, a, NG - w:NG + NL - w], ALU.add))
                    a, b = b, a
                    w *= 2
            then(dve.tensor_tensor(run[:, 0, NG + 1:], ge[:, 0:NL - 1], gt[:, 0:NL - 1], ALU.subtract), True)
            then(dve.tensor_tensor(eq, ge, gt, ALU.subtract), True)
            then(dve.tensor_reduce(need, gt, AX.X, ALU.add))
            then(dve.tensor_scalar(need, need, -1.0, float(CAP), ALU.mult, ALU.add), True)
            sums(0, 1, avail)
            then(dve.tensor_scalar(avail, avail, -1.0, need, ALU.mult, ALU.add))
            then(dve.scalar_tensor_tensor(out=avail, in0=avail, scalar=0.0, in1=eq, op0=ALU.max, op1=ALU.min))
            then(dve.tensor_tensor(run[:, 2, NG:], avail, gt, ALU.add))
            then(dve.tensor_scalar(cut[:, 1, :], run[:, 2, NG:], -1.0, float(CAP), ALU.mult, ALU.add), True)
            sums(2, 3, cut[:, 0, :])
            for half in range(2):
                then(dve.tensor_copy(of_half(cuts, half), by_list(cut, half)), half == 0)
            upto, rest = (cuts[:, i, :].rearrange("p (l a) -> p l a", a=1).broadcast_to([LP, NG, CAP])
                          for i in range(2))
            then(dve.tensor_tensor(above, slot_f[:].rearrange("p (a c) -> p a c", a=1).broadcast_to([LP, NG, CAP]),
                                   upto, ALU.is_ge))
            then(dve.tensor_tensor(above, above, rest, ALU.mult))
            then(dve.tensor_reduce(place, above.rearrange("p l c -> p c l"), AX.X, ALU.add))
            then(dve.tensor_tensor(place, place, base_f[:], ALU.add))
            assert merged[0] == MERGE_PLACE, merged[0]
            dve.wait_ge(s["exp_done"], 1)
            then(dve.reciprocal(wz[0:E, 0:1], wz[0:E, 1:2]))
            then(dve.tensor_tensor(wz[0:E, 0:1], wz[0:E, 0:1], gate[0:E, 1:2], ALU.mult))
            then(dve.tensor_copy(wz[G2:LP, 0:1], wz[0:E, 0:1]))
            assert merged[0] == MERGE_SUM, merged[0]
            dve.wait_ge(s["turn"], 1)
            dve.tensor_copy(slot_of[:], bank[0][:, 0:E]).then_inc(s["slots_ready"], 1)

            def turned(e, v):
                dve.wait_ge(s["xg_ps"], e + 1)
                dve.tensor_copy(xgT[:, v, :, :], bank[2][:, D * v:D * v + D].rearrange("p (c t) -> p c t", c=KC)
                                ).then_inc(s["xg_sb"], 1)

            def weigh(e, i):
                dve.wait_ge(s["y2_ps"], e + 1)
                dve.tensor_tensor(yb[:, i % 2, :], bank[3 - 2 * (i % 2)][:, 0:D], b2r[i][:], ALU.add
                                  ).then_inc(s["yb_done"], 1)
                dve.wait_ge(s["yb_done"], e + 1)
                if past(e, 2):
                    dve.wait_ge(s["scattered"], 16 * (e - 1))
                dve.tensor_scalar(yo[:, i % 2, :], yb[:, i % 2, :], meta[:, i, 1:2], None, ALU.mult
                                  ).then_inc(s["yo_ready"], 1)

            def expert(it, i, last):
                if not last or i + 1 < W:
                    turned(W * it + i + 1, (i + 1) % 2)
                weigh(W * it + i, i)
            turned(0, 0)
            for i in range(W):
                expert(0, i, False)
            with dve.Fori(1, LOOPS - 1) as it:
                for i in range(W):
                    expert(it, i, False)
            for i in range(W):
                expert(LOOPS - 1, i, True)

        @block.scalar
        def _(act):
            for dst, src in ((mask_row, mask.rearrange("(a b) k -> a b k", a=1).broadcast_to([P, B, NK])),
                             (mask_col[:].rearrange("p (b a) -> p b a", a=1), mask.rearrange("b (k a) -> k b a", a=1)),
                             (gate_in[:, 0:1], g_xattn.rearrange("(a b) -> a b", a=1).broadcast_to([P, 1])),
                             (gate_in[:, 1:2], g_ffn.rearrange("(a b) -> a b", a=1).broadcast_to([P, 1])),
                             (wr_sb, Wr),
                             (b1_sb, b1.rearrange("e s m -> (e s) m").rearrange("(a p) m -> p a m", a=2))):
                act.dma_start(dst, src, allow_slow_non_contiguous=True).then_inc(s["small_in"], 16)
            act.preload_act_table(ACT.Exp)
            act.wait_ge(s["small_in"], 16 * 6)
            act.activation(gate[:], gate_in[:], ACT.Tanh).then_inc(s["a_prep"], 1)
            act.wait_ge(s["p_prep"], 2)
            act.wait_ge(s["consts"], C_HEADS)
            keys = kblk[:].rearrange("p (b c) (h k) -> p b c h k", c=KC, h=HH)
            for h in range(HH):
                act.activation(keys[:, :, 1, h, :], score_ps[:, 3, 0:B * NK].rearrange("p (b k) -> p b k", b=B),
                               ACT.Copy, scale=head_of[:, h:h + 1]).then_inc(s["a_prep"], 1)

            def normalise(t, u, ln, i, to, done):
                act.activation(to[:, u:u + 1, :], xall[:, one(t, 1), :], ACT.Identity, bias=ln[3][:, i, 1:2],
                               scale=ln[3][:, i, 0:1]).then_inc(s[done], 1)

            def step(k, u):
                def turn_out(t, v, ready, src, dst, done, scale=1.0):
                    act.wait_ge(s[ready], t + 1)
                    act.activation(dst[:, v, :, :], src.rearrange("p (c t) -> p c t", c=KC), ACT.Copy, scale=scale
                                   ).then_inc(s[done], 1)

                def probs_out(g):
                    t, v = k - DLAG, (u + DLAG) % 2
                    q0, q1 = GROUPS[g]
                    act.wait_ge(s["pt_ps"], 3 * t + g + 1)
                    act.activation(probT[0:CH, v, q0:q1, :], bank[g % 2][0:CH, 0:P * (q1 - q0)]
                                   .rearrange("p (q t) -> p q t", t=P), ACT.Copy).then_inc(s["pt_sb"], 1)
                if there(k, TLAG):
                    turn_out(k - TLAG, (u + TLAG) % 2, "xT_ps", xt_ps, xT, "xT_sb")
                if there(k, DLAG):
                    probs_out(0)
                    probs_out(1)
                if there(k, TLAG):
                    turn_out(k - TLAG, (u + TLAG) % 2, "q_ps", q_psum, qT, "q_sb", DK ** -0.5)
                if there(k, DLAG):
                    probs_out(2)
                if there(k, OLAG):
                    turn_out(k - OLAG, (u + OLAG) % 2, "oT_ps", ot_ps, oT, "oT_sb")
                if there(k, GLAG):
                    t, v = k - GLAG, (u + GLAG) % 2
                    if past(t, 2):
                        act.wait_ge(s["x2T_ps"], t - 1)
                        act.wait_ge(x2_stored[v], 8 * (t - v))
                    act.wait_ge(s["rstd2"], t + 1)
                    normalise(t, v, ln2, v, x2, "x2_ready")
                if there(k, GLAG):
                    turn_out(k - GLAG, (u + GLAG) % 2, "x2T_ps", xt_ps, x2T, "x2T_sb")
                if there(k, SLAG):
                    t, v = k - SLAG, (u + SLAG) % 2
                    act.wait_ge(s["s_sub"], 2 * t + 2)
                    act.activation(prob[:, v, :], prob[:, v, :], ACT.Exp).then_inc(s["p_exp"], 1)
                if there(k, 0):
                    if past(k, 2):
                        act.wait_ge(s["xT_ps"], k - 1)
                    act.wait_ge(s["rstd1"], SETS * min(k, 8 - 1) + 1 if isinstance(k, int) and k < 8 else NT)
                    normalise(k, u, ln1, one(k, 1), xn, "xn_ready")
                if there(k, GLAG):
                    t, v = k - GLAG, (u + GLAG) % 2
                    act.wait_ge(s["lg_ps"], t + 1)
                    if past(t, 8):
                        act.wait_ge(s["loaded"], t // LT + 1)
                    j = t // 2 % 4
                    act.activation(logit[G2 * v:G2 * v + E, one(j * P, P)], lg_psum[G2 * v:G2 * v + E, :], ACT.Copy
                                   ).then_inc(s["lg_sb"], 1)
            for k in range(2 * FIRST_PAIR):
                step(k, k % 2)
            with act.Fori(FIRST_PAIR, LAST_PAIR) as n:
                for u in range(2):
                    step(2 * n + u, u)
            for k in range(NT, NT + GLAG):
                step(k, k % 2)

            act.wait_ge(s["merge"], MERGE_LIM)
            act.activation(expo, best, ACT.Exp, bias=lim[0:E, 1:2], accum_out=wz[0:E, 1:2]).then_inc(s["exp_done"], 1)
            act.activation(vexp, lval[:], ACT.Exp, bias=lim[:, 1:2]).then_inc(s["exp_done"], 1)
            act.wait_ge(s["exp_done"], 2)
            act.wait_ge(s["merge"], MERGE_SUM)
            act.activation(tab[:, :, :, 1], vexp, ACT.Copy, scale=wz[:, 0:1]).then_inc(s["exp_done"], 1)
            act.wait_ge(s["ids_done"], 2)
            act.wait_ge(s["exp_done"], 3)
            rows = table.rearrange("(e b u c) w -> u e b (c w)", e=E, b=B, u=2)
            for half in range(2):
                act.dma_start(rows[half], tab[G2 * half:G2 * half + E].rearrange("p (b h) c w -> p b (h c w)", b=B)
                              ).then_inc(s["table_stored"], 16)
            act.preload_act_table(ACT.Gelu)

            def expert(it, i):
                e = W * it + i
                for m in range(NM):
                    act.wait_ge(s["h_ps"], 2 * e + m // 4 + 1)
                    if m == 0 and past(e, 2):
                        act.wait_ge(s["y2_ps"], e - 1)
                    act.activation(hT[:, i % 2, m, :], h_psum[i % 2][:, m, :], ACT.Gelu,
                                   bias=b1T[:].rearrange("p n c -> p (n c)")[:, one(NM * e + m, 1)]
                                   ).then_inc(s["h_act"], 1)
            for i in range(W):
                expert(0, i)
            with act.Fori(1, LOOPS) as it:
                for i in range(W):
                    expert(it, i)
            act.wait_ge(s["table_stored"], 32)

        @block.tensor
        def _(pe):
            pe.wait_ge(s["ctx_in"], 16)
            pe.wait_ge(s["consts"], C_SHIFTED)
            for c in range(KC):
                for b in range(B):
                    mm = pe.transpose(score_ps[:, c, b * NK:(b + 1) * NK], ctx_sb[:, b, c * P:(c + 1) * P],
                                      ident[0:NK, 0:NK])
            mm.then_inc(s["p_prep"], 1)
            pe.wait_ge(s["v_prep"], V_CTX)
            pe.wait_ge(s["wts_in"], 64)
            for c in range(KC):
                for k in range(KC):
                    mm = pe.matmul(score_ps[:, 2 + c, 0:B * NK], wk[:, k, c * P:(c + 1) * P], ctxT[:, k, :],
                                   start=(k == 0), stop=(k == KC - 1))
            mm.then_inc(s["p_prep"], 1)
            for b in range(B):
                for k in range(KC):
                    mm = pe.matmul(bank[b][0:NK, 0:D], ctxT[:, k, b * NK:(b + 1) * NK], wv[:, k, :],
                                   start=(k == 0), stop=(k == KC - 1))
            mm.then_inc(s["p_prep"], 1)
            pe.wait_ge(s["v_prep"], V_VALUES)
            pe.wait_ge(s["a_prep"], A_KEYS)
            for q in range(KC * NCH):
                a, n, h0, nh = chunk(q % NCH)
                for h in range(nh):
                    at = CH - (NK * (h0 + h) - a)
                    mm = pe.matmul(block_ps(q)[:, :, h * DV:(h + 1) * DV], shifted[:, at:at + n],
                                   vaug[:, :, HH * (q // NCH) + h0 + h, :], start=True, stop=True)
                if q % NCH == NCH - 1:
                    mm.then_inc(s["p_prep"], 1)
            pe.wait_ge(s["small_in"], 16 * 6)
            for c in range(KC):
                pe.transpose(bank[0][:, c * E:(c + 1) * E], wr_sb[:, c * P:(c + 1) * P], ident[0:E, 0:E])
            for c in range(2):
                for a in range(2):
                    mm = pe.transpose(bank[1][:, (2 * c + a) * 2 * E:(2 * c + a + 1) * 2 * E], b1_sb[:, a, c::2],
                                      ident[0:2 * E, 0:2 * E])
            mm.then_inc(s["p_prep"], 1)

            def turn(dst, src, v, done):
                for c in range(KC):
                    mm = pe.transpose(dst[:, c * P:(c + 1) * P], src[:, v, c * P:(c + 1) * P], ident[:])
                mm.then_inc(s[done], 1)

            def turn_probs(k, u, g):
                t, v = k - DLAG, (u + DLAG) % 2
                if g == 0:
                    pe.wait_ge(s["p_exp"], t + 1)
                    if past(t, 1):
                        pe.wait_ge(s["pt_sb"], 3 * t)
                elif g == 2:
                    pe.wait_ge(s["pt_sb"], 3 * t + 1)
                q0, q1 = GROUPS[g]
                for q in range(q0, q1):
                    a, n, _, _ = chunk(q % NCH)
                    a += FLAT * (q // NCH)
                    mm = pe.transpose(bank[g % 2][0:n, (q - q0) * P:(q - q0 + 1) * P], prob[:, v, a:a + n], ident[:])
                mm.then_inc(s["pt_ps"], 1)

            def step(k, u):
                if there(k, SLAG):
                    t, v = k - SLAG, (u + SLAG) % 2
                    pe.wait_ge(s["q_sb"], t + 1)
                    if past(t, 1):
                        pe.wait_ge(s["s_sub"], 2 * t)
                    other = (t // 2 % 4 + 3) // 4 if v == 0 else 1
                    for q in (1, 2, 0):
                        if q == 0 and there(k, GLAG + 1):
                            pe.wait_ge(s["lg_sb"], k - GLAG)
                        first, n = BANKS[q][0], (BANKS[q][1] - BANKS[q][0]) * NK
                        for i, (h0, h1) in enumerate(PIECES[q]):
                            c = h0 // HH
                            pe.matmul(score_ps[:, q, (h0 - first) * NK:(h1 - first) * NK], qT[:, v, c, :],
                                      kblk[:, one(t // 8 * KC + c, 1), (h0 - c * HH) * NK:(h1 - c * HH) * NK],
                                      start=(i == 0), stop=False, skip_group_check=True)
                        mm = pe.matmul(score_ps[:, q, 0:n], ident16[:],
                                       bias_tab[:, one(t // 8 * 2 + other, 1), :].broadcast_to([P, n // NK, NK]),
                                       start=False, stop=True, skip_group_check=True)
                    mm.then_inc(s["s_ps"], 1)
                if there(k, TLAG):
                    t, v = k - TLAG, (u + TLAG) % 2
                    pe.wait_ge(s["xn_ready"], t + 1)
                    if there(k, GLAG + 1):
                        pe.wait_ge(s["x2T_sb"], k - GLAG)
                    turn(xt_ps, xn, v, "xT_ps")
                if there(k, DLAG):
                    turn_probs(k, u, 0)
                    turn_probs(k, u, 1)
                if there(k, TLAG):
                    t, v = k - TLAG, (u + TLAG) % 2
                    pe.wait_ge(s["xT_sb"], t + 1)
                    for c in range(KC):
                        for i in range(KC):
                            mm = pe.matmul(q_psum[:, c * P:(c + 1) * P], wq[:, i, c * P:(c + 1) * P], xT[:, v, i, :],
                                           start=(i == 0), stop=(i == KC - 1))
                    mm.then_inc(s["q_ps"], 1)
                if there(k, DLAG):
                    turn_probs(k, u, 2)
                if there(k, OLAG):
                    t, v = k - OLAG, (u + OLAG) % 2
                    pe.wait_ge(s["o_ready"], t + 1)
                    if past(t, 1):
                        pe.wait_ge(s["x1_ready"], t)
                    turn(ot_ps, o_sb, v, "oT_ps")
                if there(k, DLAG):
                    t, v = k - DLAG, (u + DLAG) % 2
                    pe.wait_ge(s["pt_sb"], 3 * t + 2)
                    if past(t, 1):
                        pe.wait_ge(s["o_ready"], t)
                    for q in range(KC * NCH):
                        _, n, h0, nh = chunk(q % NCH)
                        h0 += HH * (q // NCH)
                        if q == GROUPS[2][0]:
                            pe.wait_ge(s["pt_sb"], 3 * t + 3)
                        mm = pe.matmul(pv_psum[:, h0 * DV:(h0 + nh) * DV], probT[0:n, v, q, :],
                                       vblk[0:n, one(t // 8, 1), q, 0:nh * DV],
                                       start=(q == 0), stop=(q == KC * NCH - 1), skip_group_check=True)
                    mm.then_inc(s["pv_ps"], 1)
                if there(k, GLAG):
                    t, v = k - GLAG, (u + GLAG) % 2
                    pe.wait_ge(s["x2_ready"], t + 1)
                    if there(k, TLAG):
                        pe.wait_ge(s["q_sb"], k)
                    turn(xt_ps, x2, v, "x2T_ps")
                if there(k, OLAG):
                    t, v = k - OLAG, (u + OLAG) % 2
                    pe.wait_ge(s["oT_sb"], t + 1)
                    for i in range(KC):
                        mm = pe.matmul(y_psum, oT[:, v, i, :], wo[:, i, :], start=(i == 0), stop=(i == KC - 1))
                    mm.then_inc(s["y_ps"], 1)
                if there(k, GLAG):
                    t, v = k - GLAG, (u + GLAG) % 2
                    pe.wait_ge(s["x2T_sb"], t + 1)
                    if past(t, 1):
                        pe.wait_ge(s["lg_sb"], t)
                    if there(k, SLAG):
                        pe.wait_ge(s["s_sub"], 2 * (k - SLAG) + 2)
                    for i in range(KC):
                        mm = pe.matmul(lg_psum[G2 * v:G2 * v + E, :], wrT[:, i, :], x2T[:, v, i, :],
                                       start=(i == 0), stop=(i == KC - 1))
                    mm.then_inc(s["lg_ps"], 1)
            for k in range(2 * FIRST_PAIR):
                if k == SLAG:
                    pe.wait_ge(s["v_prep"], V_PARAMS)
                    pe.wait_ge(s["consts"], C_ALL)
                step(k, k % 2)
            with pe.Fori(FIRST_PAIR, LAST_PAIR) as n:
                for u in range(2):
                    step(2 * n + u, u)
            for k in range(NT, NT + GLAG):
                step(k, k % 2)

            pe.wait_ge(s["merge"], MERGE_PLACE)
            pe.matmul(bank[0][:, 0:E], place, both[:], start=True, stop=True).then_inc(s["turn"], 1)

            def turn_tokens(e, uses, i):
                pe.wait_ge(xg_in[i % 4], 16 * uses + 16)
                if past(e, 2):
                    pe.wait_ge(s["xg_sb"], e - 1)
                for c in range(KC):
                    mm = pe.transpose(bank[2][:, D * (i % 2) + c * P:D * (i % 2) + (c + 1) * P], xg[i % 4][:, c::2],
                                      ident[:])
                mm.then_inc(s["xg_ps"], 1)

            def hidden(it, i, half):
                e, v = W * it + i, i % 2
                if half == 0:
                    pe.wait_ge(s["xg_sb"], e + 1)
                    pe.wait_ge(w_in[i], 48 * it + 48)
                    if past(e, 2):
                        pe.wait_ge(s["h_act"], NM * (e - 1))
                for m in range(NM // 2 * half, NM // 2 * (half + 1)):
                    sl, c = divmod(m, 2)
                    for k in range(KC):
                        mm = pe.matmul(h_psum[v][:, m, :], w1[i][:, sl, k, c::2], xgT[:, v, k, :],
                                       start=(k == 0), stop=(k == KC - 1))
                mm.then_inc(s["h_ps"], 1)

            def output(e, i):
                v = i % 2
                if past(e, 2):
                    pe.wait_ge(s["yb_done"], e - 1)
                pe.wait_ge(s["h_act"], NM * e + NM)
                for m in range(NM):
                    sl, c = divmod(m, 2)
                    mm = pe.matmul(bank[3 - 2 * v][:, KO * sl:KO * (sl + 1)], hT[:, v, m, :],
                                   w2[i][:, sl, c, :], start=(c == 0), stop=(c == 1))
                mm.then_inc(s["y2_ps"], 1)

            def expert(it, i, last):
                e = W * it + i
                hidden(it, i, 0)
                if past(e, 1):
                    output(e - 1, (i - 1) % W)
                if not last or i + 1 < W:
                    turn_tokens(e + 1, 2 * it + (i + 1) // 4, i + 1)
                hidden(it, i, 1)
            turn_tokens(0, 0, 0)
            for i in range(W):
                expert(0, i, False)
            with pe.Fori(1, LOOPS - 1) as it:
                for i in range(W):
                    expert(it, i, False)
            for i in range(W):
                expert(LOOPS - 1, i, True)
            output(E - 1, W - 1)


_INS = ["x", "ctx_1024", "mask_BxS2_if1", "g_xattn", "g_ffn", "L0_xattn_Wq", "L0_xattn_Wk", "L0_xattn_Wv",
        "L0_xattn_Wo", "L0_ffn_Wr", "L0_ffn_W1", "L0_ffn_b1", "L0_ffn_W2", "L0_ffn_b2"]


def kernel(**inputs):
    import numpy as _np
    import concourse.bacc as _bacc
    from concourse import mybir as _mybir
    from concourse.bass_utils import run_bass_kernel_spmd as _run

    nc = _bacc.Bacc("TRN2", target_bir_lowering=False, num_devices=1)
    arrays, args = {}, []
    for name in _INS:
        a = _np.ascontiguousarray(inputs[name])
        arrays[f"in_{name}_dram"] = a
        args.append(nc.dram_tensor(f"in_{name}_dram", a.shape, _mybir.dt.from_np(a.dtype), kind="ExternalInput").ap())
    args.append(nc.dram_tensor("out_0_dram", (B, N, D), F32, kind="ExternalOutput").ap())
    build(nc, *args)
    r = _run(nc, [arrays], core_ids=[0])
    return r.results[0]["out_0_dram"]
```

```python
from contextlib import ExitStack

import concourse.bass as bass
from concourse import mybir

F32 = mybir.dt.float32
BF16 = mybir.dt.bfloat16
I32 = mybir.dt.int32
U32 = mybir.dt.uint32
ALU = mybir.AluOpType
ACT = mybir.ActivationFunctionType
AX = mybir.AxisListType
one = bass.ds

P = 128
B, N, D = 4, 1024, 256
NK = 77
H, DK = 16, 16
DV = DK + 1
E, S, M, KO = 48, 4, 256, 64
KC = D // P
TOK = B * N
NT = TOK // P
CAP = int(1.5 * TOK / E)
EPS = 1e-5
HH = H // KC
FLAT = HH * NK
BANKS = ((0, 4), (4, 10), (10, 16))
CH = 124
NCH = -(-FLAT // CH)
CHUNKS = (0, 1, 4, 2, 3)
HALF = N // 2
G2 = 64
LP = G2 + E
LT = 4
GT = LT // 2
NG = NT // LT
NL = 2 * NG
GB = NG // B
SORT = CAP.bit_length() - 1
ROUNDS = CAP // 8
RS = ROUNDS // LT
STEPS = NG * LT
W = 8
LOOPS = E // W
NM = S * 2
MASKED = 1e30
TAKEN = -3e38
GROUPS = ((0, 4), (4, 8), (8, 10))
PIECES = (((0, 4),), ((4, 8), (8, 10)), ((10, 16),))
FEW, MANY = 4, 6
PARTS = FEW + 1
TLAG, SLAG, DLAG, OLAG, GLAG = 1, 2, 3, 4, 5
FIRST_PAIR, LAST_PAIR = 4, NT // 2
SETS = NT // 8
PICK = GLAG + LT
META = 6
AHEAD = 3

ORDERING = list(enumerate((level, stage, part) for level in range(3) for stage in range(SORT + 1)
                          for part in range(2 if stage or level == 1 else 1)))

V_CTX = 1 + KC
V_KEPT = V_CTX + 9
V_VALUES = V_KEPT + 1 + B
V_KEPT_CTX = V_VALUES + KC
V_KEYS = V_KEPT_CTX + HH
V_BLOCKS = V_KEYS + NCH
V_PARAMS = V_BLOCKS + 2
C_IDENT, C_SHIFTED, C_EARLIER, C_HEADS, C_ALL = 2, 4, 6, 9, 14
C_READY = C_ALL + 11
C_MERGE = C_READY + 5
A_GATE = 1
A_KEYS = A_GATE + HH
MERGE_LIM, MERGE_SUM, MERGE_PLACE = 21, 39, 58


def chunk(i):
    a = CH * i
    n = min(CH, FLAT - a)
    return a, n, a // NK, (a + n - 1) // NK - a // NK + 1


def there(k, lag):
    return not isinstance(k, int) or 0 <= k - lag < NT


def past(t, back):
    return not isinstance(t, int) or t >= back


def stat_tiles(k):
    return [k] + [8 + (SETS - 1) * k + i for i in range(SETS - 1)] if k < 8 else []


def apart(eng, s, value):
    value = value if isinstance(value, int) else eng.to_reg(value)
    eng.wait_ge(s["ready"], 1)
    return value


def compare(dve, a, b, n, w, part):
    av, bv = (t[:, 0:n * CAP].rearrange("p (m t w) -> p m t w", t=2, w=w) for t in (a, b))
    return dve.tensor_tensor(bv[:, :, part, :], av[:, :, 0, :], av[:, :, 1, :], (ALU.max, ALU.min)[part])


def build(nc, x, ctx_in, mask, g_xattn, g_ffn, Wq, Wk, Wv, Wo, Wr, W1, b1, W2, b2, out):
    normed = nc.dram_tensor("normed", [TOK, D], F32, kind="Internal").ap()
    table = nc.dram_tensor("table", [E * NL * CAP, 2], F32, kind="Internal").ap()
    out_rows = out.rearrange("b n d -> (b n) d")
    with ExitStack() as ctx:
        def sb(name, shape, dt=F32):
            return ctx.enter_context(nc.sbuf_tensor(name, shape, dt))

        score_ps = ctx.enter_context(nc.psum_tensor("score_ps", [P, 4, 512], F32))
        bank = [ctx.enter_context(nc.psum_tensor(f"bank{i}", [P, 512], F32)) for i in range(4)]
        names = """ready ctx_in wk_in wv_in wts_in mask_in small_in consts v_prep a_prep p_prep
            stat1 aggr1 var1 rstd1 xn_ready xT_ps xT_sb q_ps q_sb s_ps top_done s_sub p_exp pt_ps pt_sb pv_ps den_done
            o_ready oT_ps oT_sb y_ps x1_ready stat2 aggr2 var2 rstd2 x2_ready x2T_ps x2T_sb lg_ps lg_sb
            loaded eight places taken filed out_stored premerge ids_done merge exp_done turn table_stored slots_ready
            picked xg_ps xg_sb h_ps h_act y2_ps yb_done yo_ready scattered""".split()
        s = {n: ctx.enter_context(nc.semaphore(n)) for n in names}
        x_in = [ctx.enter_context(nc.semaphore(f"x_in{i}")) for i in range(2 * B)]
        x2_stored = [ctx.enter_context(nc.semaphore(f"x2_stored{i}")) for i in range(2)]
        w_in = [ctx.enter_context(nc.semaphore(f"w_in{i}")) for i in range(W)]
        meta_in = [ctx.enter_context(nc.semaphore(f"meta_in{i}")) for i in range(W)]
        xg_in = [ctx.enter_context(nc.semaphore(f"xg_in{i}")) for i in range(4)]

        xall = sb("xall", [P, NT, D])
        wq, wk, wv, wo = (sb(n, [P, KC, D]) for n in ("wq", "wk", "wv", "wo"))
        kblk = sb("kblk", [P, B * KC, FLAT])
        vblk = sb("vblk", [CH, B, KC * NCH, 3 * DV])
        wrT = sb("wrT", [P, KC, E])
        b1T = sb("b1T", [P, E * S, 2])
        mask_col = sb("mask_col", [NK, B], I32)
        keep_col = sb("keep_col", [NK, B])
        causal = sb("causal", [P, NK], BF16)
        ident = sb("ident", [P, P])
        ident16 = sb("ident16", [P, P], BF16)
        head_of = sb("head_of", [P, HH])
        minus_half = sb("minus_half", [P, 1])
        gate_in = sb("gate_in", [P, 2])
        filler = sb("filler", [1, 4])
        gate = sb("gate", [P, 2])
        xn = sb("xn", [P, 2, D])
        xT = sb("xT", [P, 2, KC, P])
        qT = sb("qT", [P, 2, KC, P])
        prob = sb("prob", [P, 2, H * NK])
        probT = sb("probT", [P, 2, KC * NCH, P])
        early_t, early_p = probT[:].rearrange("p a q t -> p (a q t)"), prob[:].rearrange("p a f -> p (a f)")
        ctx_sb = early_t[0:NK, 0:B * D].rearrange("p (b d) -> p b d", b=B)
        ctxT = early_t[:, B * D:B * D + KC * B * NK].rearrange("p (c n) -> p c n", c=KC)
        vaug = early_p[0:NK, 0:B * H * DV].rearrange("p (b h d) -> p b h d", b=B, h=H)
        b1_sb = early_p[0:2 * E, B * H * DV:B * H * DV + 2 * M].rearrange("p (a m) -> p a m", a=2)
        wr_sb = early_p[0:E, B * H * DV + 2 * M:B * H * DV + 2 * M + D]
        shifted = early_p[0:NK, B * H * DV + 2 * M + D:B * H * DV + 2 * M + D + 2 * CH + NK]
        after = B * D + KC * B * NK
        kept_ctxT = early_t[:, after:after + KC * B * NK].rearrange("p (c n) -> p c n", c=KC)
        top = sb("top", [P, 2, H])
        den = sb("den", [P, 2, H])
        o_sb = sb("o_sb", [P, 2, D])
        oT = sb("oT", [P, 2, KC, P])
        x2 = sb("x2", [P, 2, D])
        x2T = sb("x2T", [P, 2, KC, P])
        ln1 = [sb(f"ln1_{n}", [P, *w]) for n, w in (("st", (SETS, 6)), ("mv", (NT, 2)), ("var", (NT, 1)),
                                                    ("rstd", (NT, 2)))]
        mask_row, keep_row, scratch, kept_of = (
            t[0:NK].rearrange(how)[:, 0:B * NK].rearrange("p (b k) -> p b k", b=B)
            for t, how in ((o_sb, "p a d -> p (a d)"), (x2, "p a d -> p (a d)"), (x2T, "p a c t -> p (a c t)"),
                           (oT, "p a c t -> p (a c t)")))
        mask_row = mask_row.bitcast(I32)
        earlier = x2[0:NK].rearrange("p a d -> p (a d)")[:, B * NK:(B + 1) * NK]
        zeros = xn[:, 1, 0:NK]
        count, first_kept = (xn[0:NK, 0, i * B:(i + 1) * B] for i in range(2))
        ln2 = [sb(f"ln2_{n}", [P, 2, w]) for n, w in (("st", 6), ("mv", 2), ("var", 1), ("rstd", 2))]
        logit = sb("logit", [LP, GB * GT * P])
        work = sb("work", [LP, 3, GT * P])
        m8 = sb("m8", [LP, 2, RS, 8])
        i8 = sb("i8", [LP, 2, RS, 8], U32)
        lval = sb("lval", [LP, NG, CAP])
        lidx = sb("lidx", [LP, NG, CAP], BF16)
        logit_by_group = logit[:].rearrange("p (h c) -> p h c", h=GB)
        lval_by_step, lidx_by_step = (a[:].rearrange("p g (s w) -> p (g s) w", s=LT) for a in (lval, lidx))
        w1 = [sb(f"w1_{i}", [P, S, KC, M]) for i in range(W)]
        w2 = [sb(f"w2_{i}", [P, S, 2, KO]) for i in range(W)]
        b2r = [sb(f"b2r_{i}", [P, D]) for i in range(W)]
        slot_of = sb("slot_of", [P, E], U32)
        pick = sb("pick", [P, W], U32)
        meta = sb("meta", [P, W, 2])
        hT = probT[:, :, 0:NM, :]
        xg = [xn[:, 0, :], xn[:, 1, :]] + [qT[:, a].rearrange("p c t -> p (c t)") for a in range(2)]
        xgT, yb, yo = xT, o_sb, x2
        listbase_i = sb("listbase_i", [LP, NG], I32)
        listbase = sb("listbase", [LP, NG])
        late = probT[0:LP].rearrange("p a q t -> p (a q t)")
        ids_f = late[:, 0:NG * CAP].rearrange("p (l c) -> p l c", l=NG)
        slot_i, base_i, slot_f, base_f = (late[:, NG * CAP + i * CAP:NG * CAP + (i + 1) * CAP] for i in range(4))
        both = sb("both", [LP, E])
        lim = sb("lim", [LP, 2])
        wz = sb("wz", [LP, 2])
        counts = sb("counts", [LP, 2, NG])
        cuts = sb("cuts", [LP, 2, NG])
        cnt = sb("cnt", [E, 2, NL])
        cut = sb("cut", [E, 2, NL])
        run = sb("run", [E, 4, NG + NL])
        small = sb("small", [E, 3, NL])
        need, avail, eq = small[:, 0, 0:1], small[:, 1, :], small[:, 2, :]
        free = kblk[0:LP].rearrange("p a f -> p (a f)")
        at = [0]

        def take(n):
            at[0] += n
            return free[:, at[0] - n:at[0]]
        above, at_least, vexp = (take(NG * CAP).rearrange("p (l c) -> p l c", l=NG) for _ in range(3))
        ahead_a, ahead_b = take(3 * CAP), take(3 * CAP)
        sort_a, sort_b = take(CAP), take(CAP)
        lower, expo, place = take(CAP)[0:E], take(CAP)[0:E], take(CAP)
        best = sort_a[0:E]
        tab = prob[0:LP].rearrange("p a f -> p (a f)")[:, 0:NG * CAP * 2].rearrange("p (l c w) -> p l c w", l=NG, w=2)
        xpairs = xall[:].rearrange("p (n u) d -> p n u d", u=2)
        xt_ps, q_psum = bank[2][:, 0:D], bank[2][:, D:2 * D]
        ot_ps, y_psum = bank[3][:, 0:D], bank[3][:, D:2 * D]
        pv_psum, lg_psum = score_ps[:, 3, 0:H * DV], score_ps[:, 0, 512 - P:]
        h_psum = [score_ps[:, 2 * v:2 * v + 2, :].rearrange("p a (m t) -> p (a m) t", t=P) for v in range(2)]

        def block_ps(i):
            _, n, _, nh = chunk(i)
            to = score_ps[0:n, i, :] if i < 4 else bank[3][0:n, :]
            return to[:, 0:KC * B * DV * nh].rearrange("p (c b w) -> p c b w", c=KC, b=B)

        block = ctx.enter_context(nc.Block())

        @block.sync
        def _(sp):
            def load_x(b, u):
                sp.dma_start(xpairs[:, 4 * b:4 * b + 4, u, :],
                             x[b, u * HALF:(u + 1) * HALF, :].rearrange("(j p) d -> p j d", p=P)
                             ).then_inc(x_in[2 * b + u], 16)

            def load_weights(e, i):
                sp.dma_start(w1[i][:], W1[one(e, 1)][0].rearrange("s (p c) m -> p s c m", c=KC)).then_inc(w_in[i], 16)
                sp.dma_start(w2[i][:], W2[one(e, 1)][0].rearrange("s (p c) k -> p s c k", c=2)).then_inc(w_in[i], 16)
                sp.dma_start(b2r[i][:], b2[one(e, 1)].rearrange("a s k -> a (s k)").broadcast_to([P, D])
                             ).then_inc(w_in[i], 16)

            def store_normed(b, j, u):
                sp.wait_ge(s["x2_ready"], 8 * b + 2 * j + u + 1)
                sp.dma_start(normed[one((8 * b + j + 4 * u) * P, P)], x2[:, u, :]).then_inc(x2_stored[u], 16)

            for dst, src, sem in ((wk, Wk, "wk_in"), (None, None, "ctx_in"), (wv, Wv, "wv_in"), (wq, Wq, "wts_in"),
                                  (wo, Wo, "wts_in")):
                if dst is None:
                    sp.dma_start(ctx_sb, ctx_in.rearrange("b k d -> k b d")).then_inc(s[sem], 16)
                else:
                    sp.dma_start(dst[:], src.rearrange("(k p) n -> p k n", p=P)).then_inc(s[sem], 16)
            load_x(0, 0)
            for i in range(1, 2 * B):
                load_x(i // 2, i % 2)
            for i in range(W):
                load_weights(i, i)
            with sp.Fori(0, B) as b:
                with sp.Fori(0, 4) as j:
                    store_normed(b, j, 0)
                    store_normed(b, j, 1)
                for u in range(2):
                    sp.dma_start(out[one(b, 1)][0][u * HALF:(u + 1) * HALF].rearrange("(j p) d -> p j d", p=P),
                                 xpairs[:, one(4 * b, 4), u, :]).then_inc(s["out_stored"], 16)
            with sp.Fori(1, LOOPS) as it:
                for i in range(W):
                    sp.wait_ge(s["y2_ps"], W * it + i - W + 1)
                    sp.wait_ge(s["yb_done"], W * it + i - W + 1)
                    load_weights(W * it + i, i)
            sp.wait_ge(s["out_stored"], 16 * 2 * B)

        @block.gpsimd
        def _(pool):
            made = [0]

            def make(ins):
                made[0] += 1
                ins.then_inc(s["consts"], 1)
                pool.wait_ge(s["consts"], made[0])

            def affine(t, compare, fill, base, pattern, channel):
                make(pool.affine_select(out=t, in_=t, compare_op=compare, fill=fill, base=base, pattern=pattern,
                                        channel_multiplier=channel))
            make(pool.memset(ident[:], 0.0))
            affine(ident[:], ALU.not_equal, 1.0, 0, [[-1, P]], 1)
            make(pool.memset(shifted, 0.0))
            affine(shifted, ALU.not_equal, 1.0, CH, [[-1, 2 * CH + NK]], 1)
            make(pool.memset(earlier, 1.0))
            affine(earlier, ALU.is_gt, 0.0, 0, [[-1, NK]], 1)
            make(pool.memset(head_of[:], 1.0))
            affine(head_of[:], ALU.is_ge, 0.0, 0, [[-DK, HH]], 1)
            affine(head_of[:], ALU.is_ge, 0.0, DK - 1, [[DK, HH]], -1)
            make(pool.memset(minus_half[:], -0.5))
            make(pool.memset(logit[:], 0.0))
            for i, (n, by) in enumerate((("filed", 4), ("taken", 1), ("loaded", 2), ("ready", 1))):
                pool.memset(filler[:, i:i + 1], 0.0).then_inc(s[n], by)
            make(pool.tensor_copy(ident16[:], ident[:]))
            make(pool.memset(zeros, 0.0))
            make(pool.affine_select(out=causal[:], in_=zeros, compare_op=ALU.is_ge, fill=MASKED, base=0,
                                    pattern=[[-1, NK]], channel_multiplier=1))
            assert made[0] == C_ALL
            make(pool.iota(listbase_i[:], pattern=[[N, B], [GT * P, GB]], base=0, channel_multiplier=0))
            make(pool.iota(listbase_i[G2:LP], pattern=[[N, B], [GT * P, GB]], base=HALF, channel_multiplier=0))
            make(pool.tensor_copy(listbase[:], listbase_i[:]))
            for t in (both, lim, wz, counts, cuts, run):
                make(pool.memset(t[:], 0.0))
            make(pool.tensor_copy(both[0:E], ident[0:E, 0:E]))
            make(pool.tensor_copy(both[G2:LP], ident[0:E, 0:E]))
            assert made[0] == C_READY

            def rstd(n, i, ln, ready, mid, done):
                _, mv, var, to = ln
                pool.wait_ge(s[ready], apart(pool, s, n + 1))
                pool.tensor_scalar(var[:, i, :], mv[:, i, 1:2], EPS, None, ALU.add).then_inc(s[mid], 1)
                pool.wait_ge(s[mid], 2 * n + 1)
                pool.tensor_tensor(to[:, i, 0:1], var[:, i, :], minus_half[:], ALU.pow).then_inc(s[mid], 1)
                pool.wait_ge(s[mid], apart(pool, s, 2 * n + 2))
                pool.tensor_scalar(to[:, i, 1:2], mv[:, i, 0:1], to[:, i, 0:1], -1.0, ALU.mult, ALU.mult
                                   ).then_inc(s[done], 1)

            def file(q, v):
                pool.wait_ge(s["places"], RS * q + RS)
                pool.tensor_copy(lval_by_step[:, one(q, 1), :], m8[:, v:v + 1].rearrange("p a r w -> p a (r w)")
                                 ).then_inc(s["filed"], 1)
                pool.tensor_copy(lidx_by_step[:, one(q, 1), :], i8[:, v:v + 1].rearrange("p a r w -> p a (r w)")
                                 ).then_inc(s["filed"], 1)

            def step(k, u):
                tiles = stat_tiles(k) if isinstance(k, int) else []
                for i, t in enumerate(tiles[0:1]):
                    rstd(SETS * k + i, t, ln1, "aggr1", "var1", "rstd1")
                if past(k, PICK + 1):
                    file(k - PICK - 1, (u + PICK + 1) % 2)
                if there(k, OLAG):
                    rstd(k - OLAG, (u + OLAG) % 2, ln2, "aggr2", "var2", "rstd2")
                for i, t in enumerate(tiles[1:], 1):
                    rstd(SETS * k + i, t, ln1, "aggr1", "var1", "rstd1")

            for k in range(PICK + 1):
                step(k, k % 2)
            with pool.Fori((PICK + 1) // 2, LAST_PAIR) as n:
                for u in range(2):
                    step(2 * n + u, u)
            for k in range(NT, NT + GLAG):
                step(k, k % 2)
            q = NT + GLAG - PICK - 1
            file(q, q % 2)
            assert q + 1 == STEPS - LT

            make(pool.iota(slot_i.bitcast(I32), pattern=[[1, CAP]], base=0, channel_multiplier=0))
            make(pool.iota(base_i.bitcast(I32), pattern=[[1, CAP]], base=0, channel_multiplier=NL * CAP))
            make(pool.memset(base_f, 0.0))
            make(pool.tensor_copy(slot_f, slot_i.bitcast(I32)))
            make(pool.tensor_copy(base_f[0:E], base_i[0:E].bitcast(I32)))
            assert made[0] == C_MERGE
            for q in range(STEPS - LT, STEPS):
                file(q, q % 2)
            pool.wait_ge(s["filed"], 2 * STEPS + 4)
            pool.tensor_tensor(ids_f, lidx[:], listbase[:].rearrange("p (l a) -> p l a", a=1)
                               .broadcast_to([LP, NG, CAP]), ALU.add).then_inc(s["ids_done"], 1)
            pool.wait_ge(s["ids_done"], 1)
            pool.tensor_copy(tab[:, :, :, 0].bitcast(U32), ids_f).then_inc(s["ids_done"], 1)

            def gather_meta(e, i):
                pool.tensor_copy(pick[:, i:i + 1], slot_of[:, one(e, 1)]).then_inc(s["picked"], 1)
                pool.wait_ge(s["picked"], apart(pool, s, e + 1))
                pool.indirect_dma_start(meta[:, i, :], None, table,
                                        bass.IndirectOffsetOnAxis(ap=pick[:, i:i + 1], axis=0)
                                        ).then_inc(meta_in[i], 16)

            def gather_tokens(e, uses, i):
                pool.wait_ge(meta_in[i], apart(pool, s, 16 * uses + 16))
                if past(e, 4):
                    pool.wait_ge(s["xg_ps"], apart(pool, s, e - 3))
                pool.indirect_dma_start(xg[i % 4], None, normed,
                                        bass.IndirectOffsetOnAxis(ap=meta[:, i, 0:1].bitcast(U32), axis=0)
                                        ).then_inc(xg_in[i % 4], 16)

            def scatter(e, i):
                pool.wait_ge(s["yo_ready"], apart(pool, s, e + 1))
                if past(e, 1):
                    pool.wait_ge(s["scattered"], apart(pool, s, 16 * e))
                pool.indirect_dma_start(out_rows, bass.IndirectOffsetOnAxis(ap=meta[:, i, 0:1].bitcast(U32), axis=0),
                                        yo[:, i % 2, :], None, compute_op=ALU.add).then_inc(s["scattered"], 16)

            def expert(it, i, last):
                e = W * it + i
                if not last or i + AHEAD < W:
                    gather_tokens(e + AHEAD, it + (i + AHEAD) // W, (i + AHEAD) % W)
                scatter(e, i)
                if not last or i + META < W:
                    gather_meta(e + META, (i + META) % W)

            pool.wait_ge(s["slots_ready"], 1)
            pool.wait_ge(s["table_stored"], 32)
            for u in range(2):
                pool.wait_ge(x2_stored[u], 16 * NT // 2)
            pool.wait_ge(s["out_stored"], 16 * 2 * B)
            for e in range(AHEAD):
                gather_meta(e, e)
            for e in range(AHEAD):
                gather_tokens(e, 0, e)
            for e in range(AHEAD, META):
                gather_meta(e, e)
            for i in range(W):
                expert(0, i, False)
            with pool.Fori(1, LOOPS - 1) as it:
                for i in range(W):
                    expert(it, i, False)
            for i in range(W):
                expert(LOOPS - 1, i, True)
            pool.wait_ge(s["scattered"], 16 * E)

        @block.vector
        def _(dve):
            prep = [0]

            def link(ins, more=False):
                prep[0] += 1
                ins.then_inc(s["v_prep"], 1)
                if not more:
                    dve.wait_ge(s["v_prep"], prep[0])
            link(dve.memset(bank[1][:], 0.0))
            dve.wait_ge(s["p_prep"], 1)
            for c in range(KC):
                link(dve.tensor_copy(ctxT[:, c, :], score_ps[:, c, 0:B * NK]), True)
            assert prep[0] == V_CTX
            dve.wait_ge(s["mask_in"], 32)
            link(dve.tensor_scalar(keep_col[:], mask_col[:], 0.0, None, ALU.not_equal), True)
            link(dve.tensor_scalar(keep_row, mask_row, 0.0, None, ALU.not_equal))
            dve.wait_ge(s["consts"], C_EARLIER)

            def wide(t, how, **sizes):
                return t.rearrange(how, **sizes).broadcast_to([NK, B, NK])
            link(dve.tensor_tensor(scratch, keep_row, wide(earlier, "p (b k) -> p b k", b=1), ALU.mult))
            link(dve.tensor_scalar(keep_row, keep_row, -1.0, 1.0, ALU.mult, ALU.add), True)
            link(dve.tensor_reduce(count, scratch, AX.X, ALU.add))
            link(dve.scalar_tensor_tensor(out=first_kept, in0=count, scalar=0.0, in1=keep_col[:], op0=ALU.is_equal,
                                          op1=ALU.mult))
            link(dve.tensor_tensor(scratch, keep_row, wide(first_kept, "p (b k) -> p b k", k=1), ALU.mult), True)
            link(dve.tensor_tensor(kept_of, wide(ident[0:NK, 0:NK], "p (b k) -> p b k", b=1),
                                   wide(keep_col[:], "p (b k) -> p b k", k=1), ALU.mult))
            link(dve.tensor_tensor(kept_of, kept_of, scratch, ALU.add), True)
            assert prep[0] == V_KEPT
            link(dve.tensor_copy(vaug[:, :, :, DK:DV], keep_col[:].rearrange("p (b h a) -> p b h a", h=1, a=1)
                                 .broadcast_to([NK, B, H, 1])), True)
            dve.wait_ge(s["p_prep"], 2)
            for b in range(B):
                link(dve.tensor_scalar(vaug[:, b, :, 0:DK], bank[b][0:NK, 0:D].rearrange("p (h d) -> p h d", h=H),
                                       keep_col[:, b:b + 1], None, ALU.mult), True)
            assert prep[0] == V_VALUES
            dve.wait_ge(s["p_prep"], 3)
            for c in range(KC):
                link(dve.tensor_copy(kept_ctxT[:, c, :], score_ps[:, c, 0:B * NK]), True)
            assert prep[0] == V_KEPT_CTX
            dve.wait_ge(s["p_prep"], 4)
            dve.wait_ge(s["consts"], C_HEADS)
            keys = kblk[:].rearrange("p (b c) (h k) -> p b c h k", c=KC, h=HH)
            for h in range(HH):
                link(dve.tensor_scalar(keys[:, :, 0, h, :], score_ps[:, 2, 0:B * NK].rearrange("p (b k) -> p b k", b=B),
                                       head_of[:, h:h + 1], None, ALU.mult), True)
            assert prep[0] == V_KEYS

            def prepare_rest():
                for n, i in enumerate(CHUNKS):
                    if n in (0, 3):
                        dve.wait_ge(s["p_prep"], 6 if n else 5)
                    _, rows, _, nh = chunk(i)
                    link(dve.tensor_copy(vblk[0:rows].rearrange("p b (c i) w -> p c b i w", c=KC)
                                         [:, :, :, i, 0:nh * DV], block_ps(i)), True)
                assert prep[0] == V_BLOCKS
                dve.wait_ge(s["p_prep"], 7)
                link(dve.tensor_copy(wrT[:], bank[0][:, 0:KC * E].rearrange("p (c e) -> p c e", c=KC)))
                link(dve.tensor_copy(b1T[:].rearrange("p n c -> p c n"),
                                     bank[1][:, 0:2 * E * S].rearrange("p (c n) -> p c n", c=2)))
                assert prep[0] == V_PARAMS
                dve.wait_ge(s["a_prep"], A_GATE)

            def load_logits(g):
                dve.wait_ge(s["lg_sb"], LT * g + LT)
                dve.wait_ge(s["places"], ROUNDS * g)
                dve.tensor_copy(work[:, 0:1, :], logit_by_group[:, one(g % GB, 1), :]).then_inc(s["loaded"], 1)

            def most_of(q, at, rr):
                r, v = RS * at + rr, at % 2
                if r == 0:
                    dve.wait_ge(s["loaded"], apart(dve, s, q // LT + 3))
                else:
                    dve.wait_ge(s["taken"], apart(dve, s, (ROUNDS - 1) * (q // LT) + r + 1))
                if rr == 0:
                    dve.wait_ge(s["filed"], apart(dve, s, 2 * q + 2))
                dve.max(m8[:, v, rr, :], work[:, r % 3, :]).then_inc(s["eight"], 1)

            def take_out(q, at, rr):
                r, v = RS * at + rr, at % 2
                if r + 1 == ROUNDS:
                    return places_of(q, at, rr)
                if r > 1:
                    dve.wait_ge(s["places"], apart(dve, s, RS * q + rr - 1))
                dve.wait_ge(s["eight"], apart(dve, s, RS * q + rr + 1))
                dve.match_replace(work[:, (r + 1) % 3, :], m8[:, v, rr, :], work[:, r % 3, :], TAKEN
                                  ).then_inc(s["taken"], 1)

            def places_of(q, at, rr):
                if rr < 0:
                    q, at, rr = q - 1, at - 1, rr + RS
                r, v = RS * at + rr, at % 2
                if r < 0:
                    return
                dve.wait_ge(s["eight"], apart(dve, s, RS * q + rr + 1))
                dve.max_index(i8[:, v, rr, :], m8[:, v, rr, :], work[:, r % 3, :]).then_inc(s["places"], 1)

            def statistics(k, places):
                for i in places:
                    if k:
                        dve.wait_ge(s["aggr1"], SETS * (k - 1) + i + 1)
                    dve.bn_stats(ln1[0][:, i, :], xall[:, stat_tiles(k)[i], :]).then_inc(s["stat1"], 1)
                for i in places:
                    dve.wait_ge(s["stat1"], SETS * k + i + 1)
                    dve.bn_aggr(ln1[1][:, stat_tiles(k)[i], :], ln1[0][:, i, :]).then_inc(s["aggr1"], 1)

            def step(k, u):
                q, at = k - PICK, (u - PICK) % LT
                picking = past(k, PICK)
                draining = isinstance(k, int) and k >= NT + SLAG
                t, v = k - SLAG, (u + SLAG) % 2
                if there(k, SLAG):
                    many = score_ps[:, 1:3, 0:MANY * NK].rearrange("p q (h k) -> p q h k", h=MANY)
                    few = score_ps[:, 0, 0:FEW * NK].rearrange("p (h k) -> p h k", h=FEW)
                    p = prob[:, v, FEW * NK:].rearrange("p (q h k) -> p q h k", q=2, h=MANY)
                    dve.wait_ge(s["s_ps"], t + 1)
                    dve.tensor_reduce(top[:, v, 0:FEW], few, AX.X, ALU.min).then_inc(s["top_done"], 1)
                if picking:
                    if at == 0:
                        load_logits(q // LT)
                    most_of(q, at, 0)
                if there(k, SLAG):
                    dve.tensor_reduce(top[:, v, FEW:].rearrange("p (q h) -> p q h", q=2), many, AX.X, ALU.min
                                      ).then_inc(s["top_done"], 1)
                if draining:
                    order_some()
                if picking:
                    take_out(q, at, 0)
                if there(k, SLAG):
                    dve.wait_ge(s["top_done"], 2 * t + 2)
                    if past(t, 2):
                        dve.wait_ge(s["pt_ps"], 3 * (t - 1))
                    dve.tensor_tensor(p, top[:, v, FEW:].rearrange("p (q h a) -> p q h a", q=2, a=1)
                                      .broadcast_to([P, 2, MANY, NK]), many, ALU.subtract).then_inc(s["s_sub"], 1)
                if draining:
                    order_some()
                if picking:
                    most_of(q, at, 1)
                    places_of(q, at, -1)
                    if draining:
                        order_some()
                    take_out(q, at, 1)
                    places_of(q, at, 0)
                    most_of(q, at, 2)
                    places_of(q, at, 1)
                    take_out(q, at, 2)
                    if draining:
                        order_some()
                t, v = k - DLAG, (u + DLAG) % 2
                if there(k, DLAG):
                    pv = pv_psum.rearrange("p (h d) -> p h d", d=DV)
                    inverse = den[:, v, :].rearrange("p (h a) -> p h a", a=1)
                    dve.wait_ge(s["pv_ps"], t + 1)
                    dve.reciprocal(inverse, pv[:, :, DK:DV]).then_inc(s["den_done"], 1)
                elif draining:
                    order_some()
                if picking:
                    most_of(q, at, 3)
                if there(k, DLAG):
                    dve.wait_ge(s["den_done"], t + 1)
                    if past(t, 2):
                        dve.wait_ge(s["oT_ps"], t - 1)
                    dve.tensor_tensor(o_sb[:, v, :].rearrange("p (h d) -> p h d", d=DK), pv[:, :, 0:DK],
                                      inverse.broadcast_to([P, H, DK]), ALU.mult).then_inc(s["o_ready"], 1)
                t, v = k - OLAG, (u + OLAG) % 2
                if there(k, OLAG):
                    dve.wait_ge(s["y_ps"], t + 1)
                    dve.scalar_tensor_tensor(out=xall[:, one(t, 1), :], in0=y_psum.rearrange("p (a d) -> p a d", a=1),
                                             scalar=gate[:, 0:1], in1=xall[:, one(t, 1), :], op0=ALU.mult,
                                             op1=ALU.add).then_inc(s["x1_ready"], 1)
                if picking:
                    places_of(q, at, 2)
                if there(k, OLAG):
                    dve.wait_ge(s["x1_ready"], apart(dve, s, t + 1))
                    dve.bn_stats(ln2[0][:, v, :], xall[:, one(t, 1), :]).then_inc(s["stat2"], 1)
                elif draining:
                    order_some()
                if picking:
                    take_out(q, at, 3)
                if there(k, OLAG):
                    dve.wait_ge(s["stat2"], apart(dve, s, t + 1))
                    dve.bn_aggr(ln2[1][:, v, :], ln2[0][:, v, :]).then_inc(s["aggr2"], 1)

            ordering = iter(ORDERING)

            def order_some():
                i, (level, stage, part) = next(ordering, (None, (None, None, None)))
                if i is None:
                    return
                if i == 0:
                    dve.wait_ge(s["filed"], 2 * (STEPS - 2 * LT) + 4)
                elif part == 0:
                    dve.wait_ge(s["premerge"], i)
                a, b = (ahead_a, ahead_b) if stage % 2 else (ahead_b, ahead_a)
                n = (3, 2, 1)[level]
                if stage:
                    ins = compare(dve, a, b, n, CAP >> stage, part)
                elif level == 0:
                    ins = dve.tensor_tensor(b[:].rearrange("p (n c) -> p n c", n=n), lval[:, 0:6:2, :],
                                            lval[:, 1:6:2, ::-1], ALU.max)
                elif part == 0:
                    ins = dve.tensor_tensor(b[:, 0:CAP], a[:, 0:CAP], a[:, CAP:2 * CAP][:, ::-1], ALU.max)
                else:
                    dve.wait_ge(s["filed"], 2 * (STEPS - LT) + 4)
                    ins = dve.tensor_tensor(b[:, CAP:2 * CAP], a[:, 2 * CAP:3 * CAP], lval[:, 6, ::-1], ALU.max)
                ins.then_inc(s["premerge"], 1)

            for k in range(3 * LT):
                if k < 8:
                    if k in (0, 2):
                        for i in (range(4), None, range(4, 2 * B))[k]:
                            dve.wait_ge(x_in[i], 16)
                    statistics(k, range(1))
                if k == 2:
                    prepare_rest()
                step(k, k % LT)
                if k < 8:
                    statistics(k, range(1, SETS))
            with dve.Fori(3, NT // LT) as n:
                for u in range(LT):
                    step(LT * n + u, u)
            for k in range(NT, NT + GLAG):
                step(k, k % LT)

            load_logits(NG - 1)
            for at in range(LT):
                for rr in range(RS):
                    q = STEPS - LT + at
                    most_of(q, at, rr)
                    places_of(q, at, rr - 1)
                    take_out(q, at, rr)
                    order_some()
                    order_some()
            assert next(ordering, None) is None

            merged = [0]

            def then(ins, more=False):
                merged[0] += 1
                ins.then_inc(s["merge"], 1)
                if not more:
                    dve.wait_ge(s["merge"], merged[0])
            dve.wait_ge(s["premerge"], len(ORDERING))
            dve.wait_ge(s["filed"], 2 * STEPS + 4)
            dve.wait_ge(s["consts"], C_MERGE)
            then(dve.tensor_tensor(sort_a, ahead_b[:, 0:CAP], lval[:, NG - 1, ::-1], ALU.max))
            for stage in range(SORT):
                for part in range(2):
                    then(compare(dve, *((sort_b, sort_a) if stage % 2 else (sort_a, sort_b)), 1, CAP >> stage + 1,
                                 part), part == 0)
            then(dve.tensor_copy(lower, sort_b[G2:LP]))
            then(dve.tensor_tensor(best, sort_b[0:E], lower[:, ::-1], ALU.max))
            then(dve.tensor_reduce(lim[0:E, 0:1], best, AX.X, ALU.min), True)
            then(dve.tensor_reduce(lim[0:E, 1:2], best, AX.X, ALU.max))
            then(dve.tensor_scalar(lim[0:E, 1:2], lim[0:E, 1:2], -1.0, None, ALU.mult))
            then(dve.tensor_copy(lim[G2:LP], lim[0:E]))
            assert merged[0] == MERGE_LIM, merged[0]
            then(dve.tensor_scalar(above, lval[:], lim[:, 0:1], None, ALU.is_gt), True)
            then(dve.tensor_scalar(at_least, lval[:], lim[:, 0:1], None, ALU.is_ge))
            then(dve.tensor_reduce(counts[:, 0, :], above, AX.X, ALU.add), True)
            then(dve.tensor_reduce(counts[:, 1, :], at_least, AX.X, ALU.add))

            def by_list(t, half):
                return t[:].rearrange("p k (b u h) -> p k b u h", b=B, u=2)[:, :, :, half, :]

            def of_half(t, half):
                return t[G2 * half:G2 * half + E].rearrange("p k (b h) -> p k b h", b=B)
            for half in range(2):
                then(dve.tensor_copy(by_list(cnt, half), of_half(counts, half)), half == 0)
            gt, ge = cnt[:, 0, :], cnt[:, 1, :]

            def sums(a, b, to):
                w = 1
                while w < NL:
                    if 2 * w == NL:
                        dst = to
                    else:
                        dst = run[:, b, NG:]
                    then(dve.tensor_tensor(dst, run[:, a, NG:], run[:, a, NG - w:NG + NL - w], ALU.add))
                    a, b = b, a
                    w *= 2
            then(dve.tensor_tensor(run[:, 0, NG + 1:], ge[:, 0:NL - 1], gt[:, 0:NL - 1], ALU.subtract), True)
            then(dve.tensor_tensor(eq, ge, gt, ALU.subtract), True)
            then(dve.tensor_reduce(need, gt, AX.X, ALU.add))
            then(dve.tensor_scalar(need, need, -1.0, float(CAP), ALU.mult, ALU.add), True)
            dve.wait_ge(s["exp_done"], 1)
            then(dve.reciprocal(wz[0:E, 0:1], wz[0:E, 1:2]), True)
            sums(0, 1, avail)
            then(dve.tensor_tensor(wz[0:E, 0:1], wz[0:E, 0:1], gate[0:E, 1:2], ALU.mult), True)
            then(dve.tensor_scalar(avail, avail, -1.0, need, ALU.mult, ALU.add))
            then(dve.tensor_copy(wz[G2:LP, 0:1], wz[0:E, 0:1]), True)
            assert merged[0] == MERGE_SUM, merged[0]
            then(dve.scalar_tensor_tensor(out=avail, in0=avail, scalar=0.0, in1=eq, op0=ALU.max, op1=ALU.min))
            then(dve.tensor_tensor(run[:, 2, NG:], avail, gt, ALU.add))
            then(dve.tensor_scalar(cut[:, 1, :], run[:, 2, NG:], -1.0, float(CAP), ALU.mult, ALU.add), True)
            sums(2, 3, cut[:, 0, :])
            for half in range(2):
                then(dve.tensor_copy(of_half(cuts, half), by_list(cut, half)), half == 0)
            for g in range(NG):
                then(dve.tensor_scalar(above[:, g, :], slot_f, cuts[:, 0, g:g + 1], cuts[:, 1, g:g + 1], ALU.is_ge,
                                       ALU.mult), g + 1 < NG)
            then(dve.tensor_reduce(place, above.rearrange("p l c -> p c l"), AX.X, ALU.add))
            then(dve.tensor_tensor(place, place, base_f, ALU.add))
            assert merged[0] == MERGE_PLACE, merged[0]
            dve.wait_ge(s["turn"], 1)
            dve.tensor_copy(slot_of[:], bank[0][:, 0:E]).then_inc(s["slots_ready"], 1)

            def turned(e, v):
                dve.wait_ge(s["xg_ps"], e + 1)
                dve.tensor_copy(xgT[:, v, :, :], bank[2][:, D * v:D * v + D].rearrange("p (c t) -> p c t", c=KC)
                                ).then_inc(s["xg_sb"], 1)

            def weigh(e, i):
                dve.wait_ge(s["y2_ps"], e + 1)
                dve.tensor_tensor(yb[:, i % 2, :], bank[3 - 2 * (i % 2)][:, 0:D], b2r[i][:], ALU.add
                                  ).then_inc(s["yb_done"], 1)
                dve.wait_ge(s["yb_done"], e + 1)
                if past(e, 2):
                    dve.wait_ge(s["scattered"], 16 * (e - 1))
                dve.tensor_scalar(yo[:, i % 2, :], yb[:, i % 2, :], meta[:, i, 1:2], None, ALU.mult
                                  ).then_inc(s["yo_ready"], 1)

            def expert(it, i, last):
                if not last or i + 1 < W:
                    turned(W * it + i + 1, (i + 1) % 2)
                weigh(W * it + i, i)
            turned(0, 0)
            for i in range(W):
                expert(0, i, False)
            with dve.Fori(1, LOOPS - 1) as it:
                for i in range(W):
                    expert(it, i, False)
            for i in range(W):
                expert(LOOPS - 1, i, True)

        @block.scalar
        def _(act):
            for dst, src, sem in (
                    (mask_row, mask.rearrange("(a b) k -> a b k", a=1).broadcast_to([NK, B, NK]), "mask_in"),
                    (mask_col[:].rearrange("p (b a) -> p b a", a=1), mask.rearrange("b (k a) -> k b a", a=1), "mask_in"),
                    (gate_in[:, 0:1], g_xattn.rearrange("(a b) -> a b", a=1).broadcast_to([P, 1]), "small_in"),
                    (gate_in[:, 1:2], g_ffn.rearrange("(a b) -> a b", a=1).broadcast_to([P, 1]), "small_in"),
                    (wr_sb, Wr, "small_in"),
                    (b1_sb, b1.rearrange("e s m -> (e s) m").rearrange("(a p) m -> p a m", a=2), "small_in")):
                act.dma_start(dst, src, allow_slow_non_contiguous=True).then_inc(s[sem], 16)
            act.preload_act_table(ACT.Exp)
            act.wait_ge(s["small_in"], 64)
            act.activation(gate[:], gate_in[:], ACT.Tanh).then_inc(s["a_prep"], 1)
            act.wait_ge(s["p_prep"], 4)
            act.wait_ge(s["consts"], C_HEADS)
            keys = kblk[:].rearrange("p (b c) (h k) -> p b c h k", c=KC, h=HH)
            for h in range(HH):
                act.activation(keys[:, :, 1, h, :], score_ps[:, 3, 0:B * NK].rearrange("p (b k) -> p b k", b=B),
                               ACT.Copy, scale=head_of[:, h:h + 1]).then_inc(s["a_prep"], 1)

            def normalise(t, u, ln, i, to, done):
                act.activation(to[:, u:u + 1, :], xall[:, one(t, 1), :], ACT.Identity, bias=ln[3][:, i, 1:2],
                               scale=ln[3][:, i, 0:1]).then_inc(s[done], 1)

            def step(k, u):
                def turn_out(t, v, ready, src, dst, done, scale=1.0):
                    act.wait_ge(s[ready], t + 1)
                    act.activation(dst[:, v, :, :], src.rearrange("p (c t) -> p c t", c=KC), ACT.Copy, scale=scale
                                   ).then_inc(s[done], 1)

                def probs_out(g):
                    t, v = k - DLAG, (u + DLAG) % 2
                    q0, q1 = GROUPS[g]
                    act.wait_ge(s["pt_ps"], 3 * t + g + 1)
                    act.activation(probT[0:CH, v, q0:q1, :], bank[g % 2][0:CH, 0:P * (q1 - q0)]
                                   .rearrange("p (q t) -> p q t", t=P), ACT.Copy).then_inc(s["pt_sb"], 1)
                if there(k, TLAG):
                    turn_out(k - TLAG, (u + TLAG) % 2, "xT_ps", xt_ps, xT, "xT_sb")
                if there(k, DLAG):
                    probs_out(0)
                    probs_out(1)
                if there(k, TLAG):
                    turn_out(k - TLAG, (u + TLAG) % 2, "q_ps", q_psum, qT, "q_sb", -DK ** -0.5)
                if there(k, DLAG):
                    probs_out(2)
                if there(k, OLAG):
                    turn_out(k - OLAG, (u + OLAG) % 2, "oT_ps", ot_ps, oT, "oT_sb")
                if there(k, SLAG):
                    t, v = k - SLAG, (u + SLAG) % 2
                    act.wait_ge(s["top_done"], 2 * t + 1)
                    if past(t, 2):
                        act.wait_ge(s["pt_ps"], 3 * (t - 1))
                    for h in range(FEW):
                        act.activation(prob[:, v, h * NK:(h + 1) * NK], score_ps[:, 0, h * NK:(h + 1) * NK], ACT.Exp,
                                       bias=top[:, v, h:h + 1], scale=-1.0).then_inc(s["p_exp"], 1)
                if there(k, GLAG):
                    t, v = k - GLAG, (u + GLAG) % 2
                    if past(t, 2):
                        act.wait_ge(s["x2T_ps"], t - 1)
                        act.wait_ge(x2_stored[v], 8 * (t - v))
                    act.wait_ge(s["rstd2"], t + 1)
                    normalise(t, v, ln2, v, x2, "x2_ready")
                if there(k, GLAG):
                    turn_out(k - GLAG, (u + GLAG) % 2, "x2T_ps", xt_ps, x2T, "x2T_sb")
                if there(k, SLAG):
                    t, v = k - SLAG, (u + SLAG) % 2
                    act.wait_ge(s["s_sub"], t + 1)
                    act.activation(prob[:, v, FEW * NK:], prob[:, v, FEW * NK:], ACT.Exp).then_inc(s["p_exp"], 1)
                if there(k, 0):
                    if past(k, 2):
                        act.wait_ge(s["xT_ps"], k - 1)
                    act.wait_ge(s["rstd1"], SETS * min(k, 8 - 1) + 1 if isinstance(k, int) and k < 8 else NT)
                    normalise(k, u, ln1, one(k, 1), xn, "xn_ready")
                if there(k, GLAG):
                    t, v = k - GLAG, (u + GLAG) % 2
                    act.wait_ge(s["lg_ps"], t + 1)
                    if past(t, 8):
                        act.wait_ge(s["loaded"], t // LT + 1)
                    j = t // 2 % 4
                    act.activation(logit[G2 * v:G2 * v + E, one(j * P, P)], lg_psum[G2 * v:G2 * v + E, :], ACT.Copy
                                   ).then_inc(s["lg_sb"], 1)
            for k in range(2 * FIRST_PAIR):
                step(k, k % 2)
            with act.Fori(FIRST_PAIR, LAST_PAIR) as n:
                for u in range(2):
                    step(2 * n + u, u)
            for k in range(NT, NT + GLAG):
                step(k, k % 2)

            act.wait_ge(s["merge"], MERGE_LIM)
            act.activation(expo, best, ACT.Exp, bias=lim[0:E, 1:2], accum_out=wz[0:E, 1:2]).then_inc(s["exp_done"], 1)
            act.activation(vexp, lval[:], ACT.Exp, bias=lim[:, 1:2]).then_inc(s["exp_done"], 1)
            act.wait_ge(s["exp_done"], 2)
            act.wait_ge(s["merge"], MERGE_SUM)
            act.activation(tab[:, :, :, 1], vexp, ACT.Copy, scale=wz[:, 0:1]).then_inc(s["exp_done"], 1)
            act.wait_ge(s["ids_done"], 2)
            act.wait_ge(s["exp_done"], 3)
            rows = table.rearrange("(e b u c) w -> u e b (c w)", e=E, b=B, u=2)
            for half in range(2):
                act.dma_start(rows[half], tab[G2 * half:G2 * half + E].rearrange("p (b h) c w -> p b (h c w)", b=B)
                              ).then_inc(s["table_stored"], 16)
            act.preload_act_table(ACT.Gelu)

            def expert(it, i):
                e = W * it + i
                for m in range(NM):
                    act.wait_ge(s["h_ps"], 2 * e + m // 4 + 1)
                    if m == 0 and past(e, 2):
                        act.wait_ge(s["y2_ps"], e - 1)
                    act.activation(hT[:, i % 2, m, :], h_psum[i % 2][:, m, :], ACT.Gelu,
                                   bias=b1T[:].rearrange("p n c -> p (n c)")[:, one(NM * e + m, 1)]
                                   ).then_inc(s["h_act"], 1)
            for i in range(W):
                expert(0, i)
            with act.Fori(1, LOOPS) as it:
                for i in range(W):
                    expert(it, i)
            act.wait_ge(s["table_stored"], 32)

        @block.tensor
        def _(pe):
            pe.wait_ge(s["ctx_in"], 16)
            pe.wait_ge(s["consts"], C_SHIFTED)
            for c in range(KC):
                for b in range(B):
                    mm = pe.transpose(score_ps[:, c, b * NK:(b + 1) * NK], ctx_sb[:, b, c * P:(c + 1) * P],
                                      ident[0:NK, 0:NK])
            mm.then_inc(s["p_prep"], 1)
            pe.wait_ge(s["v_prep"], V_CTX)
            pe.wait_ge(s["wv_in"], 16)
            for b in range(B):
                for k in range(KC):
                    mm = pe.matmul(bank[b][0:NK, 0:D], ctxT[:, k, b * NK:(b + 1) * NK], wv[:, k, :],
                                   start=(k == 0), stop=(k == KC - 1))
            mm.then_inc(s["p_prep"], 1)
            pe.wait_ge(s["v_prep"], V_KEPT)
            for c in range(KC):
                for b in range(B):
                    mm = pe.matmul(score_ps[:, c, b * NK:(b + 1) * NK], ctx_sb[:, b, c * P:(c + 1) * P],
                                   kept_of[:, b, :], start=True, stop=True)
            mm.then_inc(s["p_prep"], 1)
            pe.wait_ge(s["v_prep"], V_KEPT_CTX)
            pe.wait_ge(s["wk_in"], 16)
            for c in range(KC):
                for k in range(KC):
                    mm = pe.matmul(score_ps[:, 2 + c, 0:B * NK], wk[:, k, c * P:(c + 1) * P], kept_ctxT[:, k, :],
                                   start=(k == 0), stop=(k == KC - 1))
            mm.then_inc(s["p_prep"], 1)
            vheads = vaug.rearrange("p b (c h) d -> p c b h d", c=KC)
            for i in CHUNKS:
                a, n, h0, nh = chunk(i)
                if i == CHUNKS[3]:
                    pe.wait_ge(s["v_prep"], V_KEYS)
                    pe.wait_ge(s["a_prep"], A_KEYS)
                for h in range(nh):
                    at = CH - (NK * (h0 + h) - a)
                    mm = pe.matmul(block_ps(i)[:, :, :, h * DV:(h + 1) * DV], shifted[:, at:at + n],
                                   vheads[:, :, :, h0 + h, :], start=True, stop=True)
                if i in (CHUNKS[2], CHUNKS[-1]):
                    mm.then_inc(s["p_prep"], 1)
            pe.wait_ge(s["wts_in"], 32)
            pe.wait_ge(s["small_in"], 64)
            for c in range(KC):
                pe.transpose(bank[0][:, c * E:(c + 1) * E], wr_sb[:, c * P:(c + 1) * P], ident[0:E, 0:E])
            for c in range(2):
                for a in range(2):
                    mm = pe.transpose(bank[1][:, (2 * c + a) * 2 * E:(2 * c + a + 1) * 2 * E], b1_sb[:, a, c::2],
                                      ident[0:2 * E, 0:2 * E])
            mm.then_inc(s["p_prep"], 1)

            def turn(dst, src, v, done):
                for c in range(KC):
                    mm = pe.transpose(dst[:, c * P:(c + 1) * P], src[:, v, c * P:(c + 1) * P], ident[:])
                mm.then_inc(s[done], 1)

            def turn_probs(k, u, g):
                t, v = k - DLAG, (u + DLAG) % 2
                if g == 0:
                    pe.wait_ge(s["p_exp"], PARTS * t + PARTS)
                    if past(t, 1):
                        pe.wait_ge(s["pt_sb"], 3 * t)
                elif g == 2:
                    pe.wait_ge(s["pt_sb"], 3 * t + 1)
                q0, q1 = GROUPS[g]
                for q in range(q0, q1):
                    a, n, _, _ = chunk(q % NCH)
                    a += FLAT * (q // NCH)
                    mm = pe.transpose(bank[g % 2][0:n, (q - q0) * P:(q - q0 + 1) * P], prob[:, v, a:a + n], ident[:])
                mm.then_inc(s["pt_ps"], 1)

            def step(k, u):
                if there(k, SLAG):
                    t, v = k - SLAG, (u + SLAG) % 2
                    pe.wait_ge(s["q_sb"], t + 1)
                    if past(t, 1):
                        pe.wait_ge(s["s_sub"], t)
                    masked = u % 8 == SLAG
                    for q in (1, 2, 0):
                        if q == 0 and past(t, 1):
                            pe.wait_ge(s["p_exp"], PARTS * t - 1)
                        if q == 0 and there(k, GLAG + 1):
                            pe.wait_ge(s["lg_sb"], k - GLAG)
                        first, n = BANKS[q][0], (BANKS[q][1] - BANKS[q][0]) * NK
                        for i, (h0, h1) in enumerate(PIECES[q]):
                            c = h0 // HH
                            mm = pe.matmul(score_ps[:, q, (h0 - first) * NK:(h1 - first) * NK], qT[:, v, c, :],
                                      kblk[:, one(t // 8 * KC + c, 1), (h0 - c * HH) * NK:(h1 - c * HH) * NK],
                                      start=(i == 0), stop=(not masked and i + 1 == len(PIECES[q])),
                                      skip_group_check=True)
                        if masked:
                            mm = pe.matmul(score_ps[:, q, 0:n], ident16[:],
                                           causal[:].rearrange("p (h k) -> p h k", h=1).broadcast_to([P, n // NK, NK]),
                                           start=False, stop=True, skip_group_check=True)
                    mm.then_inc(s["s_ps"], 1)
                if there(k, TLAG):
                    t, v = k - TLAG, (u + TLAG) % 2
                    pe.wait_ge(s["xn_ready"], t + 1)
                    if there(k, GLAG + 1):
                        pe.wait_ge(s["x2T_sb"], k - GLAG)
                    turn(xt_ps, xn, v, "xT_ps")
                if there(k, DLAG):
                    turn_probs(k, u, 0)
                    turn_probs(k, u, 1)
                if there(k, TLAG):
                    t, v = k - TLAG, (u + TLAG) % 2
                    pe.wait_ge(s["xT_sb"], t + 1)
                    for c in range(KC):
                        for i in range(KC):
                            mm = pe.matmul(q_psum[:, c * P:(c + 1) * P], wq[:, i, c * P:(c + 1) * P], xT[:, v, i, :],
                                           start=(i == 0), stop=(i == KC - 1))
                    mm.then_inc(s["q_ps"], 1)
                if there(k, DLAG):
                    turn_probs(k, u, 2)
                if there(k, OLAG):
                    t, v = k - OLAG, (u + OLAG) % 2
                    pe.wait_ge(s["o_ready"], t + 1)
                    if past(t, 1):
                        pe.wait_ge(s["x1_ready"], t)
                    turn(ot_ps, o_sb, v, "oT_ps")
                if there(k, DLAG):
                    t, v = k - DLAG, (u + DLAG) % 2
                    pe.wait_ge(s["pt_sb"], 3 * t + 2)
                    if past(t, 1):
                        pe.wait_ge(s["o_ready"], t)
                    for q in range(KC * NCH):
                        _, n, h0, nh = chunk(q % NCH)
                        h0 += HH * (q // NCH)
                        if q == GROUPS[2][0]:
                            pe.wait_ge(s["pt_sb"], 3 * t + 3)
                        mm = pe.matmul(pv_psum[:, h0 * DV:(h0 + nh) * DV], probT[0:n, v, q, :],
                                       vblk[0:n, one(t // 8, 1), q, 0:nh * DV],
                                       start=(q == 0), stop=(q == KC * NCH - 1), skip_group_check=True)
                    mm.then_inc(s["pv_ps"], 1)
                if there(k, GLAG):
                    t, v = k - GLAG, (u + GLAG) % 2
                    pe.wait_ge(s["x2_ready"], t + 1)
                    if there(k, TLAG):
                        pe.wait_ge(s["q_sb"], k)
                    turn(xt_ps, x2, v, "x2T_ps")
                if there(k, OLAG):
                    t, v = k - OLAG, (u + OLAG) % 2
                    pe.wait_ge(s["oT_sb"], t + 1)
                    for i in range(KC):
                        mm = pe.matmul(y_psum, oT[:, v, i, :], wo[:, i, :], start=(i == 0), stop=(i == KC - 1))
                    mm.then_inc(s["y_ps"], 1)
                if there(k, GLAG):
                    t, v = k - GLAG, (u + GLAG) % 2
                    pe.wait_ge(s["x2T_sb"], t + 1)
                    if past(t, 1):
                        pe.wait_ge(s["lg_sb"], t)
                    if there(k, SLAG):
                        pe.wait_ge(s["p_exp"], PARTS * (k - SLAG) + FEW)
                    for i in range(KC):
                        mm = pe.matmul(lg_psum[G2 * v:G2 * v + E, :], wrT[:, i, :], x2T[:, v, i, :],
                                       start=(i == 0), stop=(i == KC - 1))
                    mm.then_inc(s["lg_ps"], 1)
            for k in range(8):
                if k == SLAG:
                    pe.wait_ge(s["v_prep"], V_PARAMS)
                    pe.wait_ge(s["consts"], C_ALL)
                step(k, k)
            with pe.Fori(1, B) as n:
                for u in range(8):
                    step(8 * n + u, u)
            for k in range(NT, NT + GLAG):
                step(k, k % 8)

            pe.wait_ge(s["merge"], MERGE_PLACE)
            pe.matmul(bank[0][:, 0:E], place, both[:], start=True, stop=True).then_inc(s["turn"], 1)

            def turn_tokens(e, uses, i):
                pe.wait_ge(xg_in[i % 4], 16 * uses + 16)
                if past(e, 2):
                    pe.wait_ge(s["xg_sb"], e - 1)
                for c in range(KC):
                    mm = pe.transpose(bank[2][:, D * (i % 2) + c * P:D * (i % 2) + (c + 1) * P], xg[i % 4][:, c::2],
                                      ident[:])
                mm.then_inc(s["xg_ps"], 1)

            def hidden(it, i, half):
                e, v = W * it + i, i % 2
                if half == 0:
                    pe.wait_ge(s["xg_sb"], e + 1)
                    pe.wait_ge(w_in[i], 48 * it + 48)
                    if past(e, 2):
                        pe.wait_ge(s["h_act"], NM * (e - 1))
                for m in range(NM // 2 * half, NM // 2 * (half + 1)):
                    sl, c = divmod(m, 2)
                    for k in range(KC):
                        mm = pe.matmul(h_psum[v][:, m, :], w1[i][:, sl, k, c::2], xgT[:, v, k, :],
                                       start=(k == 0), stop=(k == KC - 1))
                mm.then_inc(s["h_ps"], 1)

            def output(e, i):
                v = i % 2
                if past(e, 2):
                    pe.wait_ge(s["yb_done"], e - 1)
                pe.wait_ge(s["h_act"], NM * e + NM)
                for m in range(NM):
                    sl, c = divmod(m, 2)
                    mm = pe.matmul(bank[3 - 2 * v][:, KO * sl:KO * (sl + 1)], hT[:, v, m, :],
                                   w2[i][:, sl, c, :], start=(c == 0), stop=(c == 1))
                mm.then_inc(s["y2_ps"], 1)

            def expert(it, i, last):
                e = W * it + i
                hidden(it, i, 0)
                if past(e, 1):
                    output(e - 1, (i - 1) % W)
                if not last or i + 1 < W:
                    turn_tokens(e + 1, 2 * it + (i + 1) // 4, i + 1)
                hidden(it, i, 1)
            turn_tokens(0, 0, 0)
            for i in range(W):
                expert(0, i, False)
            with pe.Fori(1, LOOPS - 1) as it:
                for i in range(W):
                    expert(it, i, False)
            for i in range(W):
                expert(LOOPS - 1, i, True)
            output(E - 1, W - 1)


_INS = ["x", "ctx_1024", "mask_BxS2_if1", "g_xattn", "g_ffn", "L0_xattn_Wq", "L0_xattn_Wk", "L0_xattn_Wv",
        "L0_xattn_Wo", "L0_ffn_Wr", "L0_ffn_W1", "L0_ffn_b1", "L0_ffn_W2", "L0_ffn_b2"]


def kernel(**inputs):
    import numpy as _np
    import concourse.bacc as _bacc
    from concourse import mybir as _mybir
    from concourse.bass_utils import run_bass_kernel_spmd as _run

    nc = _bacc.Bacc("TRN2", target_bir_lowering=False, num_devices=1)
    arrays, args = {}, []
    for name in _INS:
        a = _np.ascontiguousarray(inputs[name])
        arrays[f"in_{name}_dram"] = a
        args.append(nc.dram_tensor(f"in_{name}_dram", a.shape, _mybir.dt.from_np(a.dtype), kind="ExternalInput").ap())
    args.append(nc.dram_tensor("out_0_dram", (B, N, D), F32, kind="ExternalOutput").ap())
    build(nc, *args)
    r = _run(nc, [arrays], core_ids=[0])
    return r.results[0]["out_0_dram"]
```
